# Optimizing a Trainium2 kernel written in Bass

```python
import numpy as np
import jax
import jax.numpy as jnp

def _softmax(x, axis=-1):
    return jax.nn.softmax(x, axis=axis)

def _gelu(x):
    return jax.nn.gelu(x, approximate=True)

def _silu(x):
    return jax.nn.silu(x)

def _sigmoid(x):
    return jax.nn.sigmoid(x)

def _layernorm(x, axis=-1, eps=1e-05):
    m = jnp.mean(x, axis=axis, keepdims=True)
    v = jnp.var(x, axis=axis, keepdims=True)
    return (x - m) / jnp.sqrt(v + eps)

def _scatter_add(tgt, idx, src, axis=0):
    return tgt.at[idx].add(src)

def _segment_sum(src, seg, n):
    return jax.ops.segment_sum(src, seg, n)
kernel_name = 'mk_flamingo_gated_d1_seqx_r8_827809'

def setup_inputs(seed: int=0):
    np.random.seed(seed)
    _w = jnp.asarray

    def _rec_inputs():
        import jax
        import jax.numpy as jnp
        _rk = jax.random.key(seed)
        x = 7.22e-05 + 1 * jax.random.normal(jax.random.fold_in(_rk, 1), (16, 256, 128), jnp.float32)
        _lenS = 256 - jax.random.randint(jax.random.fold_in(_rk, 7), (16,), 0, max(1, 256 // 4) + 1, jnp.int32)
        _lenS2 = 1601 - jax.random.randint(jax.random.fold_in(_rk, 8), (16,), 0, max(1, 1601 // 4) + 1, jnp.int32)
        _ctx_1024P = jax.random.normal(jax.random.fold_in(_rk, 11), (16, 16, 128), jnp.float32)
        _ctx_1024c = jax.random.dirichlet(jax.random.fold_in(_rk, 511), 0.3 * jnp.ones((16,), jnp.float32), (16, 1601))
        _ctx_1024t = jnp.einsum('bsk,bkd->bsd', _ctx_1024c, _ctx_1024P)
        _ctx_1024t = _ctx_1024t * jax.lax.rsqrt(jnp.mean(jnp.square(_ctx_1024t)) + 1e-12) * 0.953939
        ctx_1024 = -1.39393e-06 + 0.999914 * (_ctx_1024t + 0.3 * jax.random.normal(jax.random.fold_in(_rk, 611), (16, 1601, 128), jnp.float32))
        _g = jax.random.normal(jax.random.fold_in(_rk, 9001), (2, 1), jnp.float32)
        _g = jnp.sign(_g) * jnp.maximum(jnp.abs(_g), 1.0) + (_g == 0) * 1.0
        g_xattn = _g[0]
        g_ffn = _g[1]
        return (x, ctx_1024, g_xattn, g_ffn)
    x, ctx_1024, g_xattn, g_ffn = _rec_inputs()

    def _L0_xattn_setup():
        import jax, jax.numpy as jnp
        import numpy as np
        DIM = 128
        CTX_DIM = 128
        HEADS = 16
        DIM_HEAD = 64
        INNER = HEADS * DIM_HEAD
        FF_INNER = 4 * DIM
        EPS = 1e-05

        def layer_norm(x, g, b):
            mu = jnp.mean(x, axis=-1, keepdims=True)
            var = jnp.var(x, axis=-1, keepdims=True)
            return (x - mu) * jax.lax.rsqrt(var + EPS) * g + b
        key = jax.random.key(seed)
        ks = jax.random.split(key, 9)
        b, n, j = (4, 256, 128)
        inp = {'x': jax.random.normal(ks[0], (b, n, DIM), dtype=jnp.float32), 'context': jax.random.normal(ks[1], (b, j, CTX_DIM), dtype=jnp.float32), 'ln_g': jnp.ones((DIM,), jnp.float32), 'ln_b': jnp.zeros((DIM,), jnp.float32), 'cln_g': jnp.ones((CTX_DIM,), jnp.float32), 'cln_b': jnp.zeros((CTX_DIM,), jnp.float32), 'Wq': jax.random.normal(ks[2], (DIM, INNER), dtype=jnp.float32) * DIM ** (-0.5), 'Wkv': jax.random.normal(ks[3], (CTX_DIM, 2 * DIM_HEAD), dtype=jnp.float32) * CTX_DIM ** (-0.5), 'Wo': jax.random.normal(ks[4], (INNER, DIM), dtype=jnp.float32) * INNER ** (-0.5), 'Wff1': jax.random.normal(ks[5], (DIM, 2 * FF_INNER), dtype=jnp.float32) * DIM ** (-0.5), 'Wff2': jax.random.normal(ks[6], (FF_INNER, DIM), dtype=jnp.float32) * FF_INNER ** (-0.5)}
        return inp
    _L0_xattn_all = _L0_xattn_setup()
    _L0_xattn_in = {k: v for k, v in _L0_xattn_all.items() if k in ('ln_g', 'ln_b', 'cln_g', 'cln_b', 'Wq', 'Wkv', 'Wo', 'Wff1', 'Wff2')}
    del _L0_xattn_all

    def _L0_ffn_setup():
        import jax, jax.numpy as jnp
        import numpy as np
        B, S, D, H, E = (2, 256, 128, 512, 8)
        key = jax.random.key(seed)
        k0, k1, k2, k3 = jax.random.split(key, 4)
        x = jax.random.normal(k0, (B, S, D), dtype=jnp.float32)
        router_w = jax.random.normal(k1, (E, D), dtype=jnp.float32) * 0.02
        w1 = jax.random.normal(k2, (E, D, H), dtype=jnp.float32) * 0.02
        w2 = jax.random.normal(k3, (E, H, D), dtype=jnp.float32) * 0.02
        return {'x': x, 'router_w': router_w, 'w1': w1, 'w2': w2}
    _L0_ffn_all = _L0_ffn_setup()
    _L0_ffn_in = {k: v for k, v in _L0_ffn_all.items() if k in ('router_w', 'w1', 'w2')}
    del _L0_ffn_all
    return {'x': x, 'ctx_1024': ctx_1024, 'g_xattn': g_xattn, 'g_ffn': g_ffn, 'L0_xattn_ln_g': _L0_xattn_in['ln_g'], 'L0_xattn_ln_b': _L0_xattn_in['ln_b'], 'L0_xattn_cln_g': _L0_xattn_in['cln_g'], 'L0_xattn_cln_b': _L0_xattn_in['cln_b'], 'L0_xattn_Wq': _L0_xattn_in['Wq'], 'L0_xattn_Wkv': _L0_xattn_in['Wkv'], 'L0_xattn_Wo': _L0_xattn_in['Wo'], 'L0_xattn_Wff1': _L0_xattn_in['Wff1'], 'L0_xattn_Wff2': _L0_xattn_in['Wff2'], 'L0_ffn_router_w': _L0_ffn_in['router_w'], 'L0_ffn_w1': _L0_ffn_in['w1'], 'L0_ffn_w2': _L0_ffn_in['w2']}

def reference(x, ctx_1024, g_xattn, g_ffn, L0_xattn_ln_g, L0_xattn_ln_b, L0_xattn_cln_g, L0_xattn_cln_b, L0_xattn_Wq, L0_xattn_Wkv, L0_xattn_Wo, L0_xattn_Wff1, L0_xattn_Wff2, L0_ffn_router_w, L0_ffn_w1, L0_ffn_w2):
    import jax
    import jax.numpy as jnp

    def _L0_xattn_ref(x, context, ln_g, ln_b, cln_g, cln_b, Wq, Wkv, Wo, Wff1, Wff2):
        import jax, jax.numpy as jnp
        import numpy as np
        DIM = 128
        CTX_DIM = 128
        HEADS = 16
        DIM_HEAD = 64
        INNER = HEADS * DIM_HEAD
        FF_INNER = 4 * DIM
        EPS = 1e-05

        def layer_norm(x, g, b):
            mu = jnp.mean(x, axis=-1, keepdims=True)
            var = jnp.var(x, axis=-1, keepdims=True)
            return (x - mu) * jax.lax.rsqrt(var + EPS) * g + b
        scale = DIM_HEAD ** (-0.5)
        xn = layer_norm(x, ln_g, ln_b)
        cn = layer_norm(context, cln_g, cln_b)
        b, n, _ = xn.shape
        q = (xn @ Wq).reshape(b, n, HEADS, DIM_HEAD).transpose(0, 2, 1, 3) * scale
        kv = cn @ Wkv
        k, v = (kv[..., :DIM_HEAD], kv[..., DIM_HEAD:])
        sim = jnp.einsum('bhid,bjd->bhij', q, k)
        attn = jax.nn.softmax(sim, axis=-1)
        out = jnp.einsum('bhij,bjd->bhid', attn, v)
        out = out.transpose(0, 2, 1, 3).reshape(b, n, INNER) @ Wo
        ff = xn @ Wff1
        h, gate = (ff[..., :FF_INNER], ff[..., FF_INNER:])
        out = out + jax.nn.silu(gate) * h @ Wff2
        return out

    def _L0_ffn_ref(x, router_w, w1, w2):
        import jax, jax.numpy as jnp
        import numpy as np
        B, S, D, H, E = (2, 256, 128, 512, 8)
        b, s, d = x.shape
        e = router_w.shape[0]
        xf = x.reshape(-1, d)
        probs = jax.nn.softmax(xf @ router_w.T, axis=-1)
        topv, topi = jax.lax.top_k(probs, 2)
        topv = topv / (topv.sum(axis=-1, keepdims=True) + 1e-09)
        cw = (jax.nn.one_hot(topi, e, dtype=xf.dtype) * topv[..., None]).sum(axis=1)
        h = jax.nn.gelu(jnp.einsum('td,edh->teh', xf, w1), approximate=False)
        y = jnp.einsum('teh,ehd->ted', h, w2)
        out = jnp.einsum('te,ted->td', cw, y)
        return out.reshape(b, s, d)
    x = x + jnp.tanh(g_xattn[0]) * _L0_xattn_ref(_layernorm(x, axis=-1), ctx_1024, L0_xattn_ln_g, L0_xattn_ln_b, L0_xattn_cln_g, L0_xattn_cln_b, L0_xattn_Wq, L0_xattn_Wkv, L0_xattn_Wo, L0_xattn_Wff1, L0_xattn_Wff2)
    x = x + jnp.tanh(g_ffn[0]) * _L0_ffn_ref(_layernorm(x, axis=-1), L0_ffn_router_w, L0_ffn_w1, L0_ffn_w2)
    return x

_drawn_inputs = setup_inputs


def setup_inputs(seed=0):
    import zlib

    import numpy as np

    out = dict(_drawn_inputs(seed))
    spreads = {'L0_xattn_ln_g': (1.0, 0.2),
     'L0_xattn_ln_b': (0.0, 0.1),
     'L0_xattn_cln_g': (1.0, 0.2),
     'L0_xattn_cln_b': (0.0, 0.1)}
    factors = {}
    for name, (base, spread) in spreads.items():
        noise = np.random.default_rng([zlib.crc32(name.encode()), seed]).standard_normal(out[name].shape)
        drawn = base * np.exp(spread * noise) if base else spread * noise
        out[name] = jnp.asarray(drawn.astype(out[name].dtype))
    for name, factor in factors.items():
        out[name] = (out[name] * factor).astype(out[name].dtype)
    return out
```

```python
from contextlib import ExitStack

import concourse.bass as bass
from concourse import mybir

ALU = mybir.AluOpType
ACT = mybir.ActivationFunctionType
AX = mybir.AxisListType
F32 = mybir.dt.float32
F32R = mybir.dt.float32r
F16 = mybir.dt.float16

P = 128
B = 16
N = 256
J = 1601
H = 16
DH = 64
FF = 512
E = 8
EPS = 1e-5
SCALE = DH ** -0.5

TILES = B * N // P
TT = N // P
KT = -(-J // P)
KFULL = KT - 1
KLAST = J - KFULL * P
KPAD = KT * P
CH = 512
CHUNKS = B * N // CH
QCOLS = H * N
GC = 1024
G = QCOLS // GC
GT = GC // P
STEPS = G * KT
MC = 4
MCHUNKS = [(0, 400), (400, 400), (800, 400), (J - 402, 402)]
GMAX = GT * MC
PRING = 4
LAG = 2
FREE = 1
LIFT = 22.0


def keys_of(kt):
    return P if kt < KFULL else KLAST


def build(nc, x, ctx_in, g_xattn, g_ffn, ln_g, ln_b, cln_g, cln_b, Wq, Wkv, Wo, Wff1, Wff2,
          router_w, w1, w2, out):
    stack = ExitStack()
    with stack:
        def sb(name, shape, dt=F32):
            return stack.enter_context(nc.sbuf_tensor(name, shape, dt))

        def sem(name):
            return stack.enter_context(nc.semaphore(name))

        x_sb = sb("x_sb", [P, TILES, P])
        xnT = sb("xnT", [P, B * N])
        attnT = sb("attnT", [P, B * N])
        nat = attnT[:, :].rearrange("p (t d) -> p t d", d=P)
        ident = sb("ident", [P, P])
        stats = sb("stats", [P, TILES, 6])
        small = sb("small", [P, 6, TILES])
        mean, var, rstd, tmp, lnv, y0 = (small[:, i, :] for i in range(6))
        gates = sb("gates", [P, 2])
        lnw = sb("lnw", [P, 4])
        wq_sb = sb("wq_sb", [P, H, 2, DH])
        wk_sb = sb("wk_sb", [P, 2, DH])
        wv_sb = sb("wv_sb", [P, DH])
        wo_sb = sb("wo_sb", [P, H // 2, P])
        ff1_sb = sb("ff1_sb", [P, 2 * FF])
        ff2_sb = sb("ff2_sb", [P, FF // P, P])
        rwT = sb("rwT", [P, E])

        PS = stack.enter_context(nc.psum_tensor("PS", [P, 8, CH], F32))

        weights_in, x_in, ctx_in_s = sem("weights_in"), sem("x_in"), sem("ctx_loaded")
        consts_ready = sem("consts_ready")
        var_ready, rstd_guess, normed, tr_done, evac = (
            sem("var_ready"), sem("rstd_guess"), sem("normed"), sem("tr_done"), sem("evac"))
        gates_ready = sem("gates_ready")
        x_done = sem("x_done")

        def stats_to_var(dve, n, st=None):
            st = stats if st is None else st
            dve.drain()
            dve.tensor_tensor(mean[:, 0:n], st[:, 0:n, 1], st[:, 0:n, 4], ALU.add)
            dve.tensor_tensor(tmp[:, 0:n], st[:, 0:n, 1], st[:, 0:n, 4], ALU.subtract)
            dve.tensor_tensor(var[:, 0:n], st[:, 0:n, 2], st[:, 0:n, 5], ALU.add)
            dve.drain()
            dve.scalar_tensor_tensor(out=tmp[:, 0:n], in0=tmp[:, 0:n], scalar=0.25, in1=tmp[:, 0:n],
                                     op0=ALU.mult, op1=ALU.mult)
            dve.tensor_scalar(mean[:, 0:n], mean[:, 0:n], 0.5, None, ALU.mult)
            dve.tensor_scalar(var[:, 0:n], var[:, 0:n], 1.0 / P, EPS, ALU.mult, ALU.add)
            dve.drain()
            return dve.tensor_tensor(var[:, 0:n], var[:, 0:n], tmp[:, 0:n], ALU.add)

        def guess_rstd(act, n):
            nc.scalar.activation(lnv[:, 0:n], var[:, 0:n], ACT.Ln)
            act.drain()
            return nc.scalar.activation(y0[:, 0:n], lnv[:, 0:n], ACT.Exp, scale=-0.5)

        def newton(dve, n):
            dve.tensor_tensor(tmp[:, 0:n], y0[:, 0:n], y0[:, 0:n], ALU.mult)
            dve.drain()
            dve.tensor_tensor(tmp[:, 0:n], tmp[:, 0:n], var[:, 0:n], ALU.mult)
            dve.drain()
            dve.tensor_scalar(tmp[:, 0:n], tmp[:, 0:n], -0.5, 1.5, ALU.mult, ALU.add)
            dve.drain()
            dve.tensor_tensor(rstd[:, 0:n], y0[:, 0:n], tmp[:, 0:n], ALU.mult)
            dve.drain()

        with nc.Block() as block:
            @block.sync
            def _(sp):
                for c in range(4):
                    n = TILES // 4
                    sp.dma_start(x_sb[:, c * n:(c + 1) * n, :],
                                 x.rearrange("b n d -> (b n) d").rearrange("(t p) d -> p t d", p=P)
                                 [:, c * n:(c + 1) * n, :]).then_inc(x_in, 16)
                for k, v in enumerate((ln_g, ln_b, cln_g, cln_b)):
                    sp.dma_start(lnw[:, k:k + 1], v.rearrange("(d o) -> d o", o=1)).then_inc(weights_in, 16)
                for k, v in enumerate((g_xattn, g_ffn)):
                    sp.dma_start(gates[:, k:k + 1], v.rearrange("(o a) -> o a", o=1).broadcast_to([P, 1])
                                 ).then_inc(weights_in, 16)
                for k in range(2):
                    sp.dma_start(wq_sb[:, :, k, :], Wq.rearrange("d (h e) -> d h e", e=DH)).then_inc(weights_in, 16)
                    sp.dma_start(wk_sb[:, k, :], Wkv[:, 0:DH]).then_inc(weights_in, 16)
                sp.dma_start(wv_sb[:, :], Wkv[:, DH:2 * DH]).then_inc(weights_in, 16)
                sp.dma_start(wo_sb[:, :, :], Wo.rearrange("(j p) d -> p j d", p=P)).then_inc(weights_in, 16)
                sp.dma_start(ff1_sb[:, :], Wff1).then_inc(weights_in, 16)
                sp.dma_start(ff2_sb[:, :, :], Wff2.rearrange("(j p) d -> p j d", p=P)).then_inc(weights_in, 16)
                sp.dma_start(rwT[:, :], router_w).then_inc(weights_in, 16)

            @block.gpsimd
            def _(pool):
                nc.gpsimd.memset(ident[:, :], 1.0)
                pool.drain()
                nc.gpsimd.affine_select(out=ident[:, :], in_=ident[:, :], compare_op=ALU.is_equal, fill=0.0,
                                        base=0, pattern=[[-1, P]], channel_multiplier=1).then_inc(consts_ready, 1)

            @block.vector
            def _(dve):
                dve.wait_ge(x_in, 64)
                with dve.Fori(0, TILES) as t:
                    dve.bn_stats(stats[:, t, :], x_sb[:, t, :])
                stats_to_var(dve, TILES).then_inc(var_ready, 1)
                dve.wait_ge(rstd_guess, 1)
                newton(dve, TILES)
                with dve.Fori(0, TILES) as t:
                    dve.tensor_scalar(nat[:, t, :], x_sb[:, t, :], mean[:, bass.ds(t, 1)], rstd[:, bass.ds(t, 1)],
                                      ALU.subtract, ALU.mult)
                    dve.drain()
                    dve.bn_stats(stats[:, t, :], nat[:, t, :])
                stats_to_var(dve, TILES).then_inc(var_ready, 1)
                dve.wait_ge(rstd_guess, 2)
                newton(dve, TILES)
                with dve.Fori(0, TILES) as t:
                    dve.tensor_scalar(nat[:, t, :], nat[:, t, :], mean[:, bass.ds(t, 1)], rstd[:, bass.ds(t, 1)],
                                      ALU.subtract, ALU.mult).then_inc(normed, 1)

            @block.scalar
            def _(act):
                for k in range(2):
                    act.wait_ge(var_ready, k + 1)
                    guess_rstd(act, TILES).then_inc(rstd_guess, 1)
                act.wait_ge(weights_in, 16 * 15)
                for c in range(CHUNKS):
                    act.wait_ge(tr_done, c + 1)
                    nc.scalar.activation(xnT[:, c * CH:(c + 1) * CH], PS[:, c, :], ACT.Identity,
                                         scale=lnw[:, 0:1], bias=lnw[:, 1:2]).then_inc(evac, 1)
                nc.scalar.activation(gates[:, :], gates[:, :], ACT.Tanh).then_inc(gates_ready, 1)

            @block.tensor
            def _(pe):
                pe.wait_ge(consts_ready, 1)
                for c in range(CHUNKS):
                    for i in range(4):
                        pe.wait_ge(normed, 4 * c + i + 1)
                        mm = pe.transpose(PS[:, c, i * P:(i + 1) * P], nat[:, 4 * c + i, :], ident[:, :])
                    mm.then_inc(tr_done, 1)

        with ExitStack() as bstack:
            def bsb(name, shape, dt=F32):
                return bstack.enter_context(nc.sbuf_tensor(name, shape, dt))

            def bsem(name):
                return bstack.enter_context(nc.semaphore(name))

            ctx_sb = bsb("ctx_sb", [P, KT, P])
            cn = bsb("cn", [P, KT, P])
            cnT = bsb("cnT", [P, KPAD])
            K1 = bsb("K1", [P, KPAD], F32R)
            K2 = bsb("K2", [P, KPAD], F32R)
            VH = bsb("VH", [P, KT, DH + 1], F16)
            VL = bsb("VL", [P, KT, DH], F16)
            QH = bsb("QH", [P, QCOLS], F32R)
            QL = bsb("QL", [P, QCOLS], F32R)
            P32 = bsb("P32", [P, 2, GC])
            PH = bsb("PH", [P, PRING, GC], F16)
            PL = bsb("PL", [P, PRING, GC], F16)
            cm = bsb("cm", [P, GT, MC])
            mx = bsb("mx", [P, 32])
            mxT = bsb("mxT", [P, 32])
            rden = bsb("rden", [P, 2, 4])
            O_sb = bsb("O_sb", [P, TT, H * DH])
            OT = bsb("OT", [P, H // 2, N])
            kstats = bsb("kstats", [P, KT, 6])

            S = PS[:, 0:4, :]
            MX = PS[:, 4:6, :]
            O = PS[:, 6:8, :]

            ctx_loaded, ctx_used = bsem("ctx_loaded_b"), bsem("ctx_used")
            init_done = bsem("init_done")
            cvar, cguess, cnormed, ctr, cevac = (bsem("cvar"), bsem("cguess"), bsem("cnormed"),
                                                 bsem("ctr"), bsem("cevac"))
            k_mm, k_hi, k_lo = bsem("k_mm"), bsem("k_hi"), bsem("k_lo")
            v_mm, v_hi, v_lo = bsem("v_mm"), bsem("v_hi"), bsem("v_lo")
            q_mm, q_hi, q_lo = bsem("q_mm"), bsem("q_hi"), bsem("q_lo")
            max_mm, max_red, shift_ready, shift_in = (bsem("max_mm"), bsem("max_red"),
                                                      bsem("shift_ready"), bsem("shift_in"))
            scores_done, exp_done, hi_done, lo_done, pv_done, o_evac = (
                bsem("scores_done"), bsem("exp_done"), bsem("hi_done"), bsem("lo_done"),
                bsem("pv_done"), bsem("o_evac"))
            ot_tr, ot_evac, wo_mm, wo_evac = bsem("ot_tr"), bsem("ot_evac"), bsem("wo_mm"), bsem("wo_evac")

            KCH = [(j, min(CH, KPAD - j)) for j in range(0, KPAD, CH)]
            NK = len(KCH)
            VB = 7

            with nc.Block() as block:
                @block.sync
                def _(sp):
                    def load_ctx(b):
                        src = ctx_in[b, :, :] if isinstance(b, int) else ctx_in[bass.ds(b, 1), :, :].rearrange("o j d -> (o j) d")
                        sp.dma_start(ctx_sb[:, 0:KFULL, :],
                                     src[0:KFULL * P, :].rearrange("(p k) d -> p k d", k=KFULL)
                                     ).then_inc(ctx_loaded, 16)
                        sp.dma_start(ctx_sb[0:KLAST, KFULL, :], src[KFULL * P:J, :]).then_inc(ctx_loaded, 16)

                    def shift_rows(b, g):
                        sp.wait_ge(shift_ready, b * G + (g + 1))
                        for q in range(4):
                            dst = QL[DH:DH + 1, g * GC:(g + 1) * GC].bitcast(F32).rearrange(
                                "o (j r i) -> o j r i", r=4, i=32)[:, :, q, :]
                            sp.dma_start(dst, mxT[32 * q:32 * q + GT, :]).then_inc(shift_in, 16)

                    sp.wait_ge(init_done, 1)
                    sp.sem_inc(shift_in, FREE)
                    load_ctx(0)
                    with sp.Fori(0, B - 1) as b:
                        sp.wait_ge(ctx_used, b + 1)
                        load_ctx(b + 1)
                        for g in range(G):
                            shift_rows(b, g)
                    for g in range(G):
                        shift_rows(B - 1, g)

                @block.scalar
                def _(act):
                    act.sem_inc(ot_evac, FREE)
                    act.sem_inc(wo_evac, FREE)
                    with act.Fori(0, B) as b:
                        act.wait_ge(cvar, b + 1)
                        guess_rstd(act, KT).then_inc(cguess, 1)
                        for j, (c0, w) in enumerate(KCH):
                            act.wait_ge(ctr, b * NK + (j + 1))
                            nc.scalar.activation(cnT[:, c0:c0 + w], S[:, j, 0:w], ACT.Identity,
                                                 scale=lnw[:, 2:3], bias=lnw[:, 3:4]).then_inc(cevac, 1)
                        for j, (c0, w) in enumerate(KCH):
                            act.wait_ge(k_mm, b * NK + (j + 1))
                            nc.scalar.activation(K1[:, c0:c0 + w], S[:, j, 0:w], ACT.Identity)
                            nc.scalar.activation(K2[0:DH, c0:c0 + w], S[0:DH, j, 0:w],
                                                 ACT.Identity).then_inc(k_hi, 1)
                        for u, (a, z) in enumerate(((0, VB), (VB, KT))):
                            act.wait_ge(v_mm, b * 2 + (u + 1))
                            nc.scalar.activation(
                                VH[:, a:z, 0:DH], MX[:, u, 0:(z - a) * DH].rearrange("p (k d) -> p k d", d=DH),
                                ACT.Identity).then_inc(v_hi, 1)
                        for h in range(H // 2):
                            act.wait_ge(q_mm, b * (H // 2) + (h + 1))
                            nc.scalar.activation(QH[:, h * CH:(h + 1) * CH], S[:, h % 4, :],
                                                 ACT.Identity).then_inc(q_hi, 1)

                        def high_part(s):
                            kp = keys_of(s % KT)
                            act.wait_ge(exp_done, b * STEPS + (s + 1))
                            if s >= PRING:
                                act.wait_ge(pv_done, b * STEPS + (s - PRING + 1))
                            nc.scalar.activation(PH[0:kp, s % PRING, :], P32[0:kp, s % 2, :],
                                                 ACT.Identity).then_inc(hi_done, 1)

                        for s in range(STEPS):
                            kp = keys_of(s % KT)
                            act.wait_ge(scores_done, b * STEPS + (s + 1))
                            if s >= 2:
                                act.wait_ge(lo_done, b * STEPS + (s - 1))
                            nc.scalar.activation(
                                P32[0:kp, s % 2, :],
                                S[0:kp, 2 * (s % 2):2 * (s % 2) + 2, :].rearrange("p a c -> p (a c)"),
                                ACT.Exp, scale=SCALE).then_inc(exp_done, 1)
                            high_part(s)
                        for j in range(4):
                            act.wait_ge(ot_tr, b * 4 + (j + 1))
                            nc.scalar.activation(OT[:, 2 * j:2 * j + 2, :].rearrange("p a c -> p (a c)"),
                                                 S[:, j, :], ACT.Identity).then_inc(ot_evac, 1)
                        act.wait_ge(wo_mm, b + 1)
                        nc.scalar.activation(attnT[:, bass.ds(b * N, N)], MX[:, 0, 0:N],
                                             ACT.Identity).then_inc(wo_evac, 1)

                @block.vector
                def _(dve):
                    dve.wait_ge(evac, CHUNKS)
                    dve.sem_inc(o_evac, FREE)
                    dve.memset(ctx_sb[:, KFULL, :], 0.0)
                    dve.memset(QL[DH:P, :].bitcast(F32), 0.0)
                    dve.memset(K2[DH:P, :].bitcast(F32), 0.0)
                    dve.memset(VH[:, :, DH:DH + 1], 1.0)
                    dve.memset(mx[:, :], 0.0)
                    dve.drain()
                    dve.memset(K2[DH:DH + 1, :].bitcast(F32), 1.0).then_inc(init_done, 1)

                    with dve.Fori(0, B) as b:
                        dve.wait_ge(ctx_loaded, b * 32 + 32)
                        for k in range(KT):
                            dve.bn_stats(kstats[:, k, :], ctx_sb[:, k, :])
                        stats_to_var(dve, KT, kstats).then_inc(cvar, 1)
                        dve.wait_ge(cguess, b + 1)
                        newton(dve, KT)
                        for k in range(KT):
                            dve.tensor_scalar(cn[:, k, :], ctx_sb[:, k, :], mean[:, k:k + 1], rstd[:, k:k + 1],
                                              ALU.subtract, ALU.mult).then_inc(cnormed, 1)
                        dve.wait_ge(cnormed, b * KT + KT)
                        dve.sem_inc(ctx_used, 1)
                        for j, (c0, w) in enumerate(KCH):
                            dve.wait_ge(k_hi, b * NK + (j + 1))
                            dve.tensor_tensor(K1[DH:P, c0:c0 + w], S[DH:P, j, 0:w], K1[DH:P, c0:c0 + w],
                                              ALU.subtract).then_inc(k_lo, 1)
                        for u, (a, z) in enumerate(((0, VB), (VB, KT))):
                            dve.wait_ge(v_hi, b * 2 + (u + 1))
                            dve.tensor_tensor(
                                VL[:, a:z, :], MX[:, u, 0:(z - a) * DH].rearrange("p (k d) -> p k d", d=DH),
                                VH[:, a:z, 0:DH], ALU.subtract).then_inc(v_lo, 1)
                        for h in range(H // 2):
                            dve.wait_ge(q_hi, b * (H // 2) + (h + 1))
                            dve.tensor_tensor(QL[0:DH, h * CH:(h + 1) * CH], S[0:DH, h % 4, :],
                                              QH[0:DH, h * CH:(h + 1) * CH], ALU.subtract).then_inc(q_lo, 1)

                        def chunk_max(m):
                            dve.wait_ge(max_mm, b * (G * GMAX) + (m + 1))
                            w = MCHUNKS[m % MC][1]
                            dve.tensor_reduce(cm[:, m % GMAX // MC, m % MC:m % MC + 1], MX[:, m % 2, 0:w],
                                              AX.X, ALU.max).then_inc(max_red, 1)

                        def group_shift(g):
                            dve.drain()
                            dve.tensor_reduce(mx[:, 0:GT], cm[:, :, :], AX.X, ALU.max)
                            dve.drain()
                            dve.tensor_scalar(mx[:, 0:GT], mx[:, 0:GT], -1.0, LIFT, ALU.mult, ALU.add)
                            dve.drain()
                            dve.wait_ge(shift_in, FREE + (b * G + g) * 64)
                            dve.transpose(mxT[:, :], mx[:, :]).then_inc(shift_ready, 1)

                        def low_part(s):
                            kp = keys_of(s % KT)
                            dve.wait_ge(hi_done, b * STEPS + (s + 1))
                            dve.tensor_tensor(PL[0:kp, s % PRING, :], P32[0:kp, s % 2, :],
                                              PH[0:kp, s % PRING, :], ALU.subtract).then_inc(lo_done, 1)

                        def divide(g):
                            dve.wait_ge(pv_done, b * STEPS + (g + 1) * KT)
                            heads = O[:, :, 0:4 * (DH + 1)].rearrange("p u (i c) -> p u i c", c=DH + 1)
                            dve.reciprocal(rden[:, :, :], heads[:, :, :, DH])
                            dve.drain()
                            for u in range(2):
                                h0 = g * 4 + 2 * u
                                dve.tensor_tensor(
                                    O_sb[:, :, h0 * DH:(h0 + 2) * DH].rearrange("p t (h d) -> p h t d", h=2),
                                    heads[:, u, :, 0:DH].rearrange("p (h t) d -> p h t d", h=2),
                                    rden[:, u, :].rearrange("p (h t o) -> p h t o", h=2, o=1).broadcast_to([P, 2, 2, DH]),
                                    ALU.mult).then_inc(o_evac, 1)

                        for m in range(GMAX):
                            chunk_max(m)
                        group_shift(0)
                        for s in range(STEPS):
                            g, kt = divmod(s, KT)
                            if s >= 1:
                                low_part(s - 1)
                            if g + 1 < G:
                                for m in range(3 * kt, min(3 * kt + 3, GMAX)):
                                    chunk_max((g + 1) * GMAX + m)
                                if kt == (GMAX - 1) // 3:
                                    group_shift(g + 1)
                            if kt == LAG - 1 and g >= 1:
                                divide(g - 1)
                        low_part(STEPS - 1)
                        divide(G - 1)

                @block.tensor
                def _(pe):
                    pe.wait_ge(init_done, 1)
                    with pe.Fori(0, B) as b:
                        pe.wait_ge(ot_evac, FREE + b * 4)
                        for j, (c0, w) in enumerate(KCH):
                            pe.wait_ge(cnormed, b * KT + (c0 + w) // P)
                            for i in range(w // P):
                                mm = pe.transpose(S[:, j, i * P:(i + 1) * P], cn[:, c0 // P + i, :], ident[:, :])
                            mm.then_inc(ctr, 1)
                        for j, (c0, w) in enumerate(KCH):
                            pe.wait_ge(cevac, b * NK + (j + 1))
                            pe.matmul(S[:, j, 0:w], wk_sb[:, :, :].rearrange("p a e -> p (a e)"), cnT[:, c0:c0 + w],
                                      start=True, stop=True).then_inc(k_mm, 1)
                        pe.wait_ge(wo_evac, FREE + b)
                        for k in range(KT):
                            u, i = (0, k) if k < VB else (1, k - VB)
                            mm = pe.matmul(MX[:, u, i * DH:(i + 1) * DH], cnT[:, k * P:(k + 1) * P], wv_sb[:, :],
                                           start=True, stop=True)
                            if k in (VB - 1, KT - 1):
                                mm.then_inc(v_mm, 1)
                        for h in range(H // 2):
                            if h < 4:
                                pe.wait_ge(k_lo, b * NK + (h + 1))
                            else:
                                pe.wait_ge(q_lo, b * (H // 2) + (h - 3))
                            for i in range(2):
                                mm = pe.matmul(S[:, h % 4, i * N:(i + 1) * N],
                                               wq_sb[:, 2 * h + i, :, :].rearrange("p a e -> p (a e)"),
                                               xnT[:, bass.ds(b * N, N)], start=True, stop=True)
                            mm.then_inc(q_mm, 1)

                        def max_chunk(m):
                            g, r = divmod(m, GMAX)
                            c0, w = MCHUNKS[r % MC]
                            if m >= 2:
                                pe.wait_ge(max_red, b * (G * GMAX) + (m - 1))
                            col = g * GC + r // MC * P
                            pe.matmul(MX[:, m % 2, 0:w], QH[:, col:col + P], K1[:, c0:c0 + w],
                                      start=True, stop=True).then_inc(max_mm, 1)

                        def scores(s):
                            g, kt = divmod(s, KT)
                            kp = keys_of(kt)
                            if s >= 2:
                                pe.wait_ge(exp_done, b * STEPS + (s - 1))
                            if kt == 0:
                                pe.wait_ge(shift_in, FREE + (b * G + (g + 1)) * 64)
                            ks = slice(kt * P, kt * P + kp)
                            for u in range(2):
                                cols = slice(g * GC + u * CH, g * GC + (u + 1) * CH)
                                bank = S[0:kp, 2 * (s % 2) + u, :]
                                pe.matmul(bank, K1[:, ks], QH[:, cols], start=True, stop=False)
                                mm = pe.matmul(bank, K2[:, ks], QL[:, cols], start=False, stop=True)
                            mm.then_inc(scores_done, 1)

                        def weigh(s, half):
                            g, kt = divmod(s, KT)
                            kp = keys_of(kt)
                            if half == 0:
                                pe.wait_ge(lo_done, b * STEPS + (s + 1))
                                if kt == 0:
                                    pe.wait_ge(o_evac, FREE + (b * G + g) * 2)
                            for i in range(4):
                                q = slice((4 * half + i) * P, (4 * half + i + 1) * P)
                                o0 = i * (DH + 1)
                                hi, lo = PH[0:kp, s % PRING, q], PL[0:kp, s % PRING, q]
                                pe.matmul(O[:, half, o0:o0 + DH + 1], hi, VH[0:kp, kt, :],
                                          start=(kt == 0 and i == 0), stop=False, skip_group_check=True)
                                pe.matmul(O[:, half, o0:o0 + DH], hi, VL[0:kp, kt, :],
                                          start=False, stop=False, skip_group_check=True)
                                mm = pe.matmul(O[:, half, o0:o0 + DH + 1], lo, VH[0:kp, kt, :],
                                               start=False, stop=(kt == KT - 1), skip_group_check=True)
                            if half == 1:
                                mm.then_inc(pv_done, 1)

                        pe.wait_ge(k_lo, b * NK + NK)
                        pe.wait_ge(v_lo, b * 2 + 2)
                        pe.wait_ge(q_lo, b * (H // 2) + H // 2)
                        for m in range(GMAX):
                            max_chunk(m)
                        for s in range(STEPS):
                            g, kt = divmod(s, KT)
                            ms = [(g + 1) * GMAX + m for m in range(3 * kt, min(3 * kt + 3, GMAX))] if g + 1 < G else []
                            scores(s)
                            for half in range(2):
                                for m in ms[half:half + 1]:
                                    max_chunk(m)
                                if s >= LAG:
                                    weigh(s - LAG, half)
                            for m in ms[2:]:
                                max_chunk(m)
                        for s in range(STEPS - LAG, STEPS):
                            weigh(s, 0)
                            weigh(s, 1)
                        pe.wait_ge(o_evac, FREE + (b * G + G) * 2)
                        for j in range(H // 2):
                            for t in range(TT):
                                mm = pe.transpose(S[:, j // 2, (j % 2) * N + t * P:(j % 2) * N + (t + 1) * P],
                                                  O_sb[:, t, j * P:(j + 1) * P], ident[:, :])
                            if j % 2:
                                mm.then_inc(ot_tr, 1)
                        for j in range(H // 2):
                            if j % 2 == 0:
                                pe.wait_ge(ot_evac, FREE + b * 4 + (j // 2 + 1))
                            mm = pe.matmul(MX[:, 0, 0:N], wo_sb[:, j, :], OT[:, j, :],
                                           start=(j == 0), stop=(j == H // 2 - 1))
                        mm.then_inc(wo_mm, 1)

        with ExitStack() as cstack:
            def csb(name, shape, dt=F32):
                return cstack.enter_context(nc.sbuf_tensor(name, shape, dt))

            def csem(name):
                return cstack.enter_context(nc.semaphore(name))

            w1_sb = csb("w1_sb", [P, E, FF])
            w2_sb = csb("w2_sb", [P, E, FF // P, P])
            experts_in = csem("experts_in")
            silu = csb("silu", [P, FF // P, CH])
            hid = csb("hid", [P, 2, FF // P, CH])
            sumT = csb("sumT", [P, CH])
            logT = csb("logT", [E, CH])
            logits = csb("logits", [P, TILES, E])
            sel1 = csb("sel1", [P, TILES, E])
            sel2 = csb("sel2", [P, TILES, E])
            rt = csb("rt", [P, TILES, E])
            order = csb("order", [P, TILES, E])
            r1 = csb("r1", [P, TILES])
            r2 = csb("r2", [P, TILES])
            r3 = csb("r3", [P, TILES])
            cwc = csb("cwc", [P, 4, E])
            cwT = csb("cwT", [E, B * N])
            pick = csb("pick", [E, E, P])
            cwB = csb("cwB", [P, 2, CH])
            yw = csb("yw", [P, CH])
            acc = csb("acc", [P, CH])
            res = csb("res", [P, 2, 4, P])

            ff_mm, silu_done, hid_done, ff2_mm, sum_done, str_done, x1_done = (
                csem(n) for n in ("ff_mm", "silu_done", "hid_done", "ff2_mm", "sum_done", "str_done", "x1_done"))
            zvar, zguess, znormed, ztr, zevac, lt_mm, lt_evac, l_tr, l_evac = (
                csem(n) for n in ("zvar", "zguess", "znormed", "ztr", "zevac", "lt_mm", "lt_evac", "l_tr", "l_evac"))
            logits_shifted, exps_done, cw_copied, cw_tr, cw_evac, c_init = (
                csem(n) for n in ("logits_shifted", "exps_done", "cw_copied", "cw_tr", "cw_evac", "c_init"))
            h_mm, h_gelu, y_mm, y_used, b_mm, b_evac, acc_done, acc_tr, res_done, stored = (
                csem(n) for n in ("h_mm", "h_gelu", "y_mm", "y_used", "b_mm", "b_evac", "acc_done", "acc_tr",
                                  "res_done", "stored"))
            NB = FF // P

            with nc.Block() as block:
                @block.gpsimd
                def _(pool):
                    nc.gpsimd.memset(pick[:, :, :], 1.0)
                    for e in range(E):
                        nc.gpsimd.memset(order[:, :, e:e + 1], float(E - e))
                    pool.drain()
                    nc.gpsimd.affine_select(out=pick[:, :, :], in_=pick[:, :, :], compare_op=ALU.is_equal, fill=0.0,
                                            base=0, pattern=[[-1, E], [0, P]], channel_multiplier=1).then_inc(c_init, 1)

                @block.tensor
                def _(pe):
                    pe.sem_inc(y_mm, FREE)
                    pe.sem_inc(cw_tr, FREE)
                    pe.sem_inc(acc_tr, FREE)
                    with pe.Fori(0, CHUNKS) as c:
                        cols = xnT[:, bass.ds(c * CH, CH)]
                        pe.wait_ge(x1_done, FREE + c)
                        for j in [j for k in range(NB) for j in (NB + k, k)]:
                            pe.matmul(PS[:, j, :], ff1_sb[:, j * P:(j + 1) * P], cols,
                                      start=True, stop=True).then_inc(ff_mm, 1)
                        for k in range(NB):
                            pe.wait_ge(hid_done, FREE + c * NB + (k + 1))
                            mm = pe.matmul(PS[:, NB, :], ff2_sb[:, k, :], hid[:, 0, k, :],
                                           start=(k == 0), stop=(k == NB - 1))
                        mm.then_inc(ff2_mm, 1)
                        pe.wait_ge(sum_done, c + 1)
                        for i in range(4):
                            mm = pe.transpose(PS[:, NB + 1, i * P:(i + 1) * P], sumT[:, i * P:(i + 1) * P], ident[:, :])
                        mm.then_inc(str_done, 1)
                    for c in range(CHUNKS):
                        pe.wait_ge(znormed, 4 * c + 4)
                        if c >= 2:
                            pe.wait_ge(zevac, c - 1)
                        for i in range(4):
                            mm = pe.transpose(PS[:, c % 2, i * P:(i + 1) * P], nat[:, 4 * c + i, :], ident[:, :])
                        mm.then_inc(ztr, 1)
                        pe.wait_ge(zevac, c + 1)
                        if c >= 1:
                            pe.wait_ge(lt_evac, c)
                        pe.matmul(PS[0:E, 2, :], rwT[:, :], xnT[:, c * CH:(c + 1) * CH],
                                  start=True, stop=True).then_inc(lt_mm, 1)
                        pe.wait_ge(lt_evac, c + 1)
                        if c >= 1:
                            pe.wait_ge(l_evac, c)
                        for i in range(4):
                            mm = pe.transpose(PS[:, 3, i * E:(i + 1) * E], logT[:, i * P:(i + 1) * P], ident[0:E, 0:E])
                        mm.then_inc(l_tr, 1)
                    with pe.Fori(0, CHUNKS) as c:
                        pe.wait_ge(cw_copied, c + 1)
                        pe.wait_ge(cw_evac, FREE + c)
                        for i in range(4):
                            mm = pe.transpose(PS[0:E, 4, i * P:(i + 1) * P], cwc[:, i, :], ident[:, :])
                        mm.then_inc(cw_tr, 1)
                    pe.wait_ge(c_init, 1)
                    pe.wait_ge(experts_in, 32)
                    pe.wait_ge(cw_evac, FREE + CHUNKS)
                    with pe.Fori(0, CHUNKS) as c:
                        def expert_in(e):
                            for k in range(NB):
                                pe.wait_ge(h_gelu, FREE + c * (E * NB) + (max(e - 1, 0) * NB + k + 1 if e else 0))
                                pe.matmul(PS[:, k, :], w1_sb[:, e, k * P:(k + 1) * P], xnT[:, bass.ds(c * CH, CH)],
                                          start=True, stop=True).then_inc(h_mm, 1)

                        def expert_out(e):
                            if e >= 2:
                                pe.wait_ge(y_used, FREE + c * E + (e - 1))
                            for k in range(NB):
                                if k == NB - 1:
                                    pe.wait_ge(b_evac, FREE + c * E + e)
                                pe.wait_ge(h_gelu, FREE + c * (E * NB) + (e * NB + k + 1))
                                mm = pe.matmul(PS[:, 4 + e % 2, :], w2_sb[:, e, k, :], hid[:, e % 2, k, :],
                                               start=(k == 0), stop=(k == NB - 1))
                            mm.then_inc(y_mm, 1)
                            pe.matmul(PS[:, 6, :], pick[:, e, :], cwT[:, bass.ds(c * CH, CH)],
                                      start=True, stop=True).then_inc(b_mm, 1)

                        pe.wait_ge(y_used, FREE + c * E)
                        for e in range(E):
                            expert_in(e)
                            if e >= 1:
                                expert_out(e - 1)
                        expert_out(E - 1)
                        pe.wait_ge(acc_done, c + 1)
                        pe.wait_ge(res_done, FREE + c)
                        for i in range(4):
                            mm = pe.transpose(PS[:, 7, i * P:(i + 1) * P], acc[:, i * P:(i + 1) * P], ident[:, :])
                        mm.then_inc(acc_tr, 1)

                @block.scalar
                def _(act):
                    act.sem_inc(h_gelu, FREE)
                    act.sem_inc(b_evac, FREE)
                    act.sem_inc(cw_evac, FREE)
                    with act.Fori(0, CHUNKS) as c:
                        for k in range(NB):
                            act.wait_ge(ff_mm, c * (2 * NB) + (2 * k + 1))
                            if k == 0:
                                act.wait_ge(hid_done, FREE + c * NB)
                            nc.scalar.activation(silu[:, k, :], PS[:, NB + k, :], ACT.Silu).then_inc(silu_done, 1)
                    act.wait_ge(zvar, 1)
                    guess_rstd(act, TILES).then_inc(zguess, 1)
                    for c in range(CHUNKS):
                        act.wait_ge(ztr, c + 1)
                        nc.scalar.activation(xnT[:, c * CH:(c + 1) * CH], PS[:, c % 2, :],
                                             ACT.Identity).then_inc(zevac, 1)
                        act.wait_ge(lt_mm, c + 1)
                        if c >= 1:
                            act.wait_ge(l_tr, c)
                        nc.scalar.activation(logT[:, :], PS[0:E, 2, :], ACT.Identity).then_inc(lt_evac, 1)
                    act.wait_ge(logits_shifted, 1)
                    nc.scalar.activation(logits[:, :, :], logits[:, :, :], ACT.Exp).then_inc(exps_done, 1)
                    with act.Fori(0, CHUNKS) as c:
                        act.wait_ge(cw_tr, FREE + c + 1)
                        nc.scalar.activation(cwT[:, bass.ds(c * CH, CH)], PS[0:E, 4, :], ACT.Identity).then_inc(cw_evac, 1)
                    with act.Fori(0, CHUNKS) as c:
                        for e in range(E):
                            for k in range(NB):
                                act.wait_ge(h_mm, c * (E * NB) + (e * NB + k + 1))
                                if k == 0:
                                    act.wait_ge(y_mm, FREE + c * E + (e - 1 if e >= 2 else 0))
                                nc.scalar.activation(hid[:, e % 2, k, :], PS[:, k, :], ACT.Gelu).then_inc(h_gelu, 1)
                            if e >= 1:
                                act.wait_ge(b_mm, c * E + e)
                                if e >= 3:
                                    act.wait_ge(y_used, FREE + c * E + (e - 2))
                                else:
                                    act.wait_ge(y_used, FREE + c * E)
                                nc.scalar.activation(cwB[:, (e - 1) % 2, :], PS[:, 6, :], ACT.Identity).then_inc(b_evac, 1)
                        act.wait_ge(b_mm, c * E + E)
                        act.wait_ge(y_used, FREE + c * E + (E - 2))
                        nc.scalar.activation(cwB[:, (E - 1) % 2, :], PS[:, 6, :], ACT.Identity).then_inc(b_evac, 1)

                @block.vector
                def _(dve):
                    dve.wait_ge(gates_ready, 1)
                    dve.sem_inc(y_used, FREE)
                    dve.sem_inc(res_done, FREE)
                    dve.sem_inc(x1_done, FREE)
                    dve.sem_inc(hid_done, FREE)
                    with dve.Fori(0, CHUNKS) as c:
                        for k in range(NB):
                            dve.wait_ge(silu_done, c * NB + (k + 1))
                            dve.wait_ge(ff_mm, c * (2 * NB) + (2 * k + 2))
                            dve.tensor_tensor(hid[:, 0, k, :], silu[:, k, :], PS[:, k, :],
                                              ALU.mult).then_inc(hid_done, 1)
                        dve.wait_ge(ff2_mm, c + 1)
                        dve.tensor_tensor(sumT[:, :], PS[:, NB, :], attnT[:, bass.ds(c * CH, CH)],
                                          ALU.add).then_inc(sum_done, 1)
                        dve.wait_ge(str_done, c + 1)
                        rows = x_sb[:, bass.ds(c * 4, 4), :]
                        dve.scalar_tensor_tensor(out=rows, in0=PS[:, NB + 1, :].rearrange("p (t d) -> p t d", d=P),
                                                 scalar=gates[:, 0:1], in1=rows,
                                                 op0=ALU.mult, op1=ALU.add).then_inc(x1_done, 1)
                        dve.drain()
                        for i in range(4):
                            dve.bn_stats(stats[:, bass.ds(c * 4 + i, 1), :].rearrange("p o k -> p (o k)"),
                                         x_sb[:, bass.ds(c * 4 + i, 1), :].rearrange("p o k -> p (o k)"))
                    stats_to_var(dve, TILES).then_inc(zvar, 1)
                    dve.wait_ge(zguess, 1)
                    newton(dve, TILES)
                    with dve.Fori(0, TILES) as t:
                        dve.tensor_scalar(nat[:, t, :], x_sb[:, t, :], mean[:, bass.ds(t, 1)], rstd[:, bass.ds(t, 1)],
                                          ALU.subtract, ALU.mult).then_inc(znormed, 1)
                    with dve.Fori(0, CHUNKS) as c:
                        dve.wait_ge(l_tr, c + 1)
                        dve.tensor_copy(logits[:, bass.ds(c * 4, 4), :],
                                        PS[:, 3, 0:4 * E].rearrange("p (t e) -> p t e", e=E)).then_inc(l_evac, 1)
                    dve.drain()

                    def spread(v):
                        return v[:, :].rearrange("p (t o) -> p t o", o=1).broadcast_to([P, TILES, E])

                    dve.tensor_reduce(r1[:, :], logits[:, :, :], AX.X, ALU.max)
                    dve.drain()
                    dve.tensor_tensor(logits[:, :, :], logits[:, :, :], spread(r1), ALU.subtract).then_inc(logits_shifted, 1)
                    dve.wait_ge(exps_done, 1)
                    dve.wait_ge(c_init, 1)
                    dve.tensor_reduce(r1[:, :], logits[:, :, :], AX.X, ALU.add)
                    dve.drain()
                    dve.reciprocal(r2[:, :], r1[:, :])
                    dve.drain()
                    dve.tensor_tensor(rt[:, :, :], logits[:, :, :], spread(r2), ALU.mult)
                    dve.drain()

                    def top(best, sel):
                        dve.tensor_reduce(best[:, :], rt[:, :, :], AX.X, ALU.max)
                        dve.drain()
                        dve.tensor_tensor(sel[:, :, :], rt[:, :, :], spread(best), ALU.is_equal)
                        dve.drain()
                        dve.tensor_tensor(sel[:, :, :], sel[:, :, :], order[:, :, :], ALU.mult)
                        dve.drain()
                        dve.tensor_reduce(r3[:, :], sel[:, :, :], AX.X, ALU.max)
                        dve.drain()
                        dve.tensor_tensor(sel[:, :, :], sel[:, :, :], spread(r3), ALU.is_equal)
                        dve.drain()

                    top(r1, sel1)
                    dve.scalar_tensor_tensor(out=rt[:, :, :], in0=sel1[:, :, :], scalar=-4.0, in1=rt[:, :, :],
                                             op0=ALU.mult, op1=ALU.add)
                    dve.drain()
                    top(r2, sel2)
                    dve.tensor_tensor(r3[:, :], r1[:, :], r2[:, :], ALU.add)
                    dve.tensor_tensor(sel1[:, :, :], sel1[:, :, :], spread(r1), ALU.mult)
                    dve.tensor_tensor(sel2[:, :, :], sel2[:, :, :], spread(r2), ALU.mult)
                    dve.drain()
                    dve.tensor_scalar(r3[:, :], r3[:, :], 1e-9, None, ALU.add)
                    dve.tensor_tensor(sel1[:, :, :], sel1[:, :, :], sel2[:, :, :], ALU.add)
                    dve.drain()
                    dve.reciprocal(r3[:, :], r3[:, :])
                    dve.drain()
                    dve.tensor_tensor(sel1[:, :, :], sel1[:, :, :], spread(r3), ALU.mult)
                    dve.drain()
                    with dve.Fori(0, CHUNKS) as c:
                        dve.wait_ge(cw_tr, FREE + c)
                        dve.tensor_copy(cwc[:, :, :], sel1[:, bass.ds(c * 4, 4), :]).then_inc(cw_copied, 1)
                    with dve.Fori(0, CHUNKS) as c:
                        dve.wait_ge(acc_tr, FREE + c)
                        for e in range(E):
                            dve.wait_ge(y_mm, FREE + c * E + (e + 1))
                            dve.wait_ge(b_evac, FREE + c * E + (e + 1))
                            dst = acc if e == 0 else yw
                            ins = dve.tensor_tensor(dst[:, :], PS[:, 4 + e % 2, :], cwB[:, e % 2, :],
                                                    ALU.mult)
                            ins.then_inc(y_used, 1)
                            dve.drain()
                            if e:
                                ins = dve.tensor_tensor(acc[:, :], acc[:, :], yw[:, :], ALU.add)
                                if e == E - 1:
                                    ins.then_inc(acc_done, 1)
                                dve.drain()
                        dve.wait_ge(acc_tr, FREE + c + 1)
                        dve.wait_ge(stored, FREE + c * 16)
                        dve.scalar_tensor_tensor(out=res[:, 0, :, :], in0=PS[:, 7, :].rearrange("p (t d) -> p t d", d=P),
                                                 scalar=gates[:, 1:2], in1=x_sb[:, bass.ds(c * 4, 4), :],
                                                 op0=ALU.mult, op1=ALU.add).then_inc(res_done, 1)

                @block.sync
                def _(sp):
                    sp.dma_start(w1_sb[:, :, :], w1.rearrange("e d h -> d e h")).then_inc(experts_in, 16)
                    sp.dma_start(w2_sb[:, :, :, :], w2.rearrange("e (j p) d -> p e j d", p=P)).then_inc(experts_in, 16)
                    rows = out.rearrange("b n d -> (b n) d").rearrange("(t p) d -> p t d", p=P)
                    sp.sem_inc(stored, FREE)
                    with sp.Fori(0, CHUNKS) as c:
                        sp.wait_ge(res_done, FREE + c + 1)
                        sp.dma_start(rows[:, bass.ds(c * 4, 4), :], res[:, 0, :, :]).then_inc(stored, 16)
                    sp.wait_ge(stored, FREE + 16 * CHUNKS)


_INS = ['x', 'ctx_1024', 'g_xattn', 'g_ffn', 'L0_xattn_ln_g', 'L0_xattn_ln_b', 'L0_xattn_cln_g', 'L0_xattn_cln_b',
        'L0_xattn_Wq', 'L0_xattn_Wkv', 'L0_xattn_Wo', 'L0_xattn_Wff1', 'L0_xattn_Wff2', 'L0_ffn_router_w',
        'L0_ffn_w1', 'L0_ffn_w2']


def kernel(**inputs):
    import numpy as _np
    import concourse.bacc as _bacc
    from concourse import mybir as _mybir
    from concourse.bass_utils import run_bass_kernel_spmd as _run

    nc = _bacc.Bacc("TRN2", target_bir_lowering=False, num_devices=1)
    arrays, args = {}, []
    for name in _INS:
        a = _np.ascontiguousarray(inputs[name].T if name == 'L0_ffn_router_w' else inputs[name])
        arrays[f"in_{name}_dram"] = a
        args.append(nc.dram_tensor(f"in_{name}_dram", a.shape, _mybir.dt.from_np(a.dtype), kind="ExternalInput").ap())
    args.append(nc.dram_tensor("out_0_dram", (16, 256, 128), _mybir.dt.float32, kind="ExternalOutput").ap())
    build(nc, *args)
    r = _run(nc, [arrays], core_ids=[0])
    return r.results[0]["out_0_dram"]
```

```python
from contextlib import ExitStack

import concourse.bass as bass
from concourse import mybir

ALU = mybir.AluOpType
ACT = mybir.ActivationFunctionType
AX = mybir.AxisListType
F32 = mybir.dt.float32
F32R = mybir.dt.float32r
F16 = mybir.dt.float16
I32 = mybir.dt.int32

P = 128
B = 16
N = 256
J = 1601
H = 16
DH = 64
FF = 512
E = 8
EPS = 1e-5
SCALE = DH ** -0.5

TILES = B * N // P
TT = N // P
KT = -(-J // P)
KFULL = KT - 1
KLAST = J - KFULL * P
KPAD = KT * P
CH = 512
CHUNKS = B * N // CH
QCOLS = H * N
GC = 1024
G = QCOLS // GC
GT = GC // P
STEPS = G * KT
MC = 4
MCHUNKS = [(0, 400), (400, 400), (800, 400), (J - 402, 402)]
GMAX = GT * MC
PRING = 4
LAG = 2
FREE = 1
LIFT = 22.0


def keys_of(kt):
    return P if kt < KFULL else KLAST


def build(nc, x, ctx_in, g_xattn, g_ffn, ln_g, ln_b, cln_g, cln_b, Wq, Wkv, Wo, Wff1, Wff2,
          router_w, w1, w2, out):
    stack = ExitStack()
    with stack:
        def sb(name, shape, dt=F32):
            return stack.enter_context(nc.sbuf_tensor(name, shape, dt))

        def sem(name):
            return stack.enter_context(nc.semaphore(name))

        x_sb = sb("x_sb", [P, TILES, P])
        xnT = sb("xnT", [P, B * N])
        attnT = sb("attnT", [P, B * N])
        nat = attnT[:, :].rearrange("p (t d) -> p t d", d=P)
        ident = sb("ident", [P, P])
        stats = sb("stats", [P, TILES, 6])
        small = sb("small", [P, 6, TILES])
        mean, var, rstd, tmp, lnv, y0 = (small[:, i, :] for i in range(6))
        gates = sb("gates", [P, 2])
        lnw = sb("lnw", [P, 4])
        wq_sb = sb("wq_sb", [P, H * DH])
        wkv_sb = sb("wkv_sb", [P, 2 * DH])
        ident16 = sb("ident16", [P, P], F16)
        bound = sb("bound", [P, 2])
        vscale = sb("vscale", [P, 2])
        wo_sb = sb("wo_sb", [P, H // 2, P])
        ff1_sb = sb("ff1_sb", [P, 2 * FF])
        ff2_sb = sb("ff2_sb", [P, FF // P, P])
        rwT = sb("rwT", [P, E])

        PS = stack.enter_context(nc.psum_tensor("PS", [P, 8, CH], F32))

        weights_in, x_in = sem("weights_in"), sem("x_in")
        consts_ready = sem("consts_ready")
        normed, tr_done, evac = sem("normed"), sem("tr_done"), sem("evac")
        gates_ready, bounds_ready = sem("gates_ready"), sem("bounds_ready")

        def stats_to_var(dve, n, st=None):
            st = stats if st is None else st
            dve.drain()
            dve.tensor_tensor(mean[:, 0:n], st[:, 0:n, 1], st[:, 0:n, 4], ALU.add)
            dve.tensor_tensor(tmp[:, 0:n], st[:, 0:n, 1], st[:, 0:n, 4], ALU.subtract)
            dve.tensor_tensor(var[:, 0:n], st[:, 0:n, 2], st[:, 0:n, 5], ALU.add)
            dve.drain()
            dve.scalar_tensor_tensor(out=tmp[:, 0:n], in0=tmp[:, 0:n], scalar=0.25, in1=tmp[:, 0:n],
                                     op0=ALU.mult, op1=ALU.mult)
            dve.tensor_scalar(mean[:, 0:n], mean[:, 0:n], 0.5, None, ALU.mult)
            dve.tensor_scalar(var[:, 0:n], var[:, 0:n], 1.0 / P, EPS, ALU.mult, ALU.add)
            dve.drain()
            return dve.tensor_tensor(var[:, 0:n], var[:, 0:n], tmp[:, 0:n], ALU.add)

        def inverse_root(dve, n):
            y = rstd[:, 0:n]
            dve.tensor_scalar(tmp[:, 0:n].bitcast(I32), var[:, 0:n].bitcast(I32), 1, None, ALU.logical_shift_right)
            dve.drain()
            dve.tensor_scalar(y.bitcast(I32), tmp[:, 0:n].bitcast(I32), -1.0, float(0x5F3759DF), ALU.mult, ALU.add)
            dve.drain()
            for _ in range(3):
                dve.tensor_tensor(tmp[:, 0:n], y, y, ALU.mult)
                dve.drain()
                dve.scalar_tensor_tensor(out=tmp[:, 0:n], in0=tmp[:, 0:n], scalar=-0.5, in1=var[:, 0:n],
                                         op0=ALU.mult, op1=ALU.mult)
                dve.drain()
                dve.scalar_tensor_tensor(out=y, in0=tmp[:, 0:n], scalar=1.5, in1=y, op0=ALU.add, op1=ALU.mult)
                dve.drain()

        with nc.Block() as block:
            @block.sync
            def _(sp):
                for c in range(4):
                    n = TILES // 4
                    sp.dma_start(x_sb[:, c * n:(c + 1) * n, :],
                                 x.rearrange("b n d -> (b n) d").rearrange("(t p) d -> p t d", p=P)
                                 [:, c * n:(c + 1) * n, :]).then_inc(x_in, 16)
                for k, v in enumerate((ln_g, ln_b, cln_g, cln_b)):
                    sp.dma_start(lnw[:, k:k + 1], v.rearrange("(d o) -> d o", o=1)).then_inc(weights_in, 16)
                for k, v in enumerate((g_xattn, g_ffn)):
                    sp.dma_start(gates[:, k:k + 1], v.rearrange("(o a) -> o a", o=1).broadcast_to([P, 1])
                                 ).then_inc(weights_in, 16)
                sp.dma_start(wkv_sb[:, :], Wkv).then_inc(weights_in, 16)
                sp.dma_start(wq_sb[:, :], Wq).then_inc(weights_in, 16)
                sp.dma_start(wo_sb[:, :, :], Wo.rearrange("(j p) d -> p j d", p=P)).then_inc(weights_in, 16)
                sp.dma_start(ff1_sb[:, :], Wff1).then_inc(weights_in, 16)
                sp.dma_start(ff2_sb[:, :, :], Wff2.rearrange("(j p) d -> p j d", p=P)).then_inc(weights_in, 16)
                sp.dma_start(rwT[:, :], router_w).then_inc(weights_in, 16)

            @block.gpsimd
            def _(pool):
                nc.gpsimd.memset(ident[:, :], 1.0)
                pool.drain()
                nc.gpsimd.affine_select(out=ident[:, :], in_=ident[:, :], compare_op=ALU.is_equal, fill=0.0,
                                        base=0, pattern=[[-1, P]], channel_multiplier=1).then_inc(consts_ready, 1)
                pool.wait_ge(bounds_ready, 1)
                nc.gpsimd.partition_all_reduce(vscale[:, :], bound[:, :], P, bass.bass_isa.ReduceOp.max).then_inc(bounds_ready, 1)

            @block.vector
            def _(dve):
                dve.wait_ge(x_in, 64)
                with dve.Fori(0, TILES // 4) as c:
                    for k in range(4):
                        dve.bn_stats(stats[:, c * 4 + k, :], x_sb[:, c * 4 + k, :])
                stats_to_var(dve, TILES)
                dve.drain()
                inverse_root(dve, TILES)
                with dve.Fori(0, TILES // 4) as c:
                    for k in range(4):
                        dve.tensor_scalar(nat[:, c * 4 + k, :], x_sb[:, c * 4 + k, :], mean[:, bass.ds(c * 4 + k, 1)],
                                          rstd[:, bass.ds(c * 4 + k, 1)], ALU.subtract, ALU.mult)
                    dve.drain()
                    for k in range(4):
                        dve.bn_stats(stats[:, c * 4 + k, :], nat[:, c * 4 + k, :])
                stats_to_var(dve, TILES)
                dve.drain()
                inverse_root(dve, TILES)
                with dve.Fori(0, TILES // 4) as c:
                    for k in range(4):
                        ins = dve.tensor_scalar(nat[:, c * 4 + k, :], nat[:, c * 4 + k, :], mean[:, bass.ds(c * 4 + k, 1)],
                                                rstd[:, bass.ds(c * 4 + k, 1)], ALU.subtract, ALU.mult)
                    ins.then_inc(normed, 1)
                dve.wait_ge(weights_in, 16 * 12)
                dve.wait_ge(consts_ready, 1)
                dve.tensor_copy(ident16[:, :], ident[:, :])
                dve.tensor_reduce(bound[:, 0:1], wkv_sb[:, DH:2 * DH], AX.X, ALU.max, apply_absolute_value=True)
                dve.tensor_reduce(bound[:, 1:2], lnw[:, 2:4], AX.X, ALU.max, apply_absolute_value=True)
                dve.drain()
                dve.sem_inc(bounds_ready, 1)
                dve.wait_ge(bounds_ready, 2)
                dve.tensor_scalar(vscale[:, :], vscale[:, :], 1e-15, None, ALU.max)
                dve.drain()
                dve.tensor_tensor(vscale[:, 0:1], vscale[:, 0:1], vscale[:, 1:2], ALU.mult)
                dve.drain()
                dve.reciprocal(vscale[:, 1:2], vscale[:, 0:1])
                dve.drain()
                dve.tensor_scalar(wkv_sb[:, DH:2 * DH], wkv_sb[:, DH:2 * DH], vscale[:, 1:2], None, ALU.mult)
                dve.tensor_scalar(wo_sb[:, :, :], wo_sb[:, :, :], vscale[:, 0:1], None, ALU.mult)

            @block.scalar
            def _(act):
                act.wait_ge(weights_in, 16 * 12)
                for c in range(CHUNKS):
                    act.wait_ge(tr_done, c + 1)
                    nc.scalar.activation(xnT[:, c * CH:(c + 1) * CH], PS[:, c, :], ACT.Identity,
                                         scale=lnw[:, 0:1], bias=lnw[:, 1:2]).then_inc(evac, 1)
                nc.scalar.activation(gates[:, :], gates[:, :], ACT.Tanh).then_inc(gates_ready, 1)

            @block.tensor
            def _(pe):
                pe.wait_ge(consts_ready, 1)
                for c in range(CHUNKS):
                    pe.wait_ge(normed, c + 1)
                    for i in range(4):
                        mm = pe.transpose(PS[:, c, i * P:(i + 1) * P], nat[:, 4 * c + i, :], ident[:, :])
                    mm.then_inc(tr_done, 1)

        with ExitStack() as bstack:
            def bsb(name, shape, dt=F32):
                return bstack.enter_context(nc.sbuf_tensor(name, shape, dt))

            def bsem(name):
                return bstack.enter_context(nc.semaphore(name))

            ctx_sb = bsb("ctx_sb", [P, KT, P])
            cn = bsb("cn", [P, KT, P])
            cnT = bsb("cnT", [P, KPAD])
            K1 = [bsb(f"K1_{i}", [P, KPAD], F32R) for i in range(2)]
            K2 = [bsb(f"K2_{i}", [P, KPAD], F32R) for i in range(2)]
            VT = bsb("VT", [P, KPAD], F16)
            VH = bsb("VH", [P, 2, KT, DH + 1], F16)
            VL = bsb("VL", [P, 2, KT, DH], F16)
            QH = bsb("QH", [P, QCOLS], F32R)
            QL = bsb("QL", [P, QCOLS], F32R)
            P32 = bsb("P32", [P, 2, CH])
            PH = bsb("PH", [P, PRING, GC], F16)
            PL = bsb("PL", [P, PRING, GC], F16)
            cm = bsb("cm", [P, GT, MC])
            mx = bsb("mx", [P, 32])
            mxT = bsb("mxT", [P, 32])
            rden = bsb("rden", [P, 2, 4])
            O_sb = bsb("O_sb", [P, 2, TT, G * DH])
            OT = bsb("OT", [P, H // 2, N])
            kstats = bsb("kstats", [P, KT, 6])

            S = PS[:, 0:4, :]
            MX = PS[:, 4:6, :]
            O = PS[:, 6:8, :]

            ctx_loaded, ctx_used, init_done, cnormed = (
                bsem(n) for n in ("ctx_loaded", "ctx_used", "init_done", "cnormed"))
            job_mm = bsem("job_mm")
            bank_free = [bsem(f"bank_free_{i}") for i in range(2)]
            k_hi, v_hi, v_lo, v_ready = (
                bsem(n) for n in ("k_hi", "v_hi", "v_lo", "v_ready"))
            q_hi, shift_ready, shift_in = (
                bsem(n) for n in ("q_hi", "shift_ready", "shift_in"))
            q_dup = [bsem(f"q_dup_{i}") for i in range(2)]
            scores_done, exp_done, hi_done, lo_dve, lo_pool, pv_done, o_evac = (
                bsem(n) for n in ("scores_done", "exp_done", "hi_done", "lo_dve", "lo_pool", "pv_done",
                                  "o_evac"))

            KCH = [(j, min(CH, KPAD - j)) for j in range(0, KPAD, CH)]
            NK = len(KCH)
            VSPLIT = [(0, 7), (7, KT)]
            PAIRS = B // 2

            def prep_jobs(p):
                return ([[("t", p, j) for j in range(NK)], [("kv", p, j) for j in range(NK)],
                         [("vt", p, u) for u in range(2)]])

            PROLOGUE = ([j for part in prep_jobs(0) for j in part] + [("q", 0, 0), ("q", 1, 0)]
                        + [("max", 0, m) for m in range(GMAX)])

            def plan(last):
                at = [[] for _ in range(2 * STEPS + 1)]
                for r in range(2 * G):
                    p, g = divmod(r, G)
                    ahead = not (last and r >= G)
                    side = [("q", r + 2, 0)] if not (last and r + 2 >= 2 * G) else []
                    if ahead and g < 3:
                        side += prep_jobs(1 - p)[g]
                    if g == 0 and p == 1:
                        side.append(("wo", 0, 0))
                    maxes = [("max", r + 1, m) for m in range(GMAX)] if not (last and r == 2 * G - 1) else []
                    per = 3 if r < 2 * G - 1 else 2
                    steps = [[] for _ in range(KT)]
                    for kt in range(KT):
                        if kt == 3 and r >= 1:
                            steps[kt].append(("otr", r - 1, 0))
                        while len(steps[kt]) < per and maxes:
                            steps[kt].append(maxes.pop(0))
                        if r == 2 * G - 1 and kt >= 4 and side:
                            steps[kt].append(side.pop(0))
                        while len(steps[kt]) < per and side:
                            steps[kt].append(side.pop(0))
                    steps[KT - 1] += side
                    for kt in range(KT):
                        at[r * KT + kt] = steps[kt]
                    if r == 2 * G - 1:
                        at[2 * STEPS] = maxes + [("otr", r, 0), ("wo", 1, 0)]
                return at

            SIDE = {last: plan(last) for last in (False, True)}
            JOBS = sum(map(len, SIDE[False]))
            assert JOBS % 2 == 0 and len(PROLOGUE) % 2 == 0

            def numbered(last):
                n, out_ = 0, []
                for jobs in SIDE[last]:
                    out_.append([(job, n + k) for k, job in enumerate(jobs)])
                    n += len(jobs)
                return out_

            def job_count(i, n):
                return i * JOBS + (len(PROLOGUE) + n + 1)

            def freed(i, n):
                return i * (JOBS // 2) + (len(PROLOGUE) + n) // 2

            with nc.Block() as block:
                @block.sync
                def _(sp):
                    def load_ctx(b):
                        src = ctx_in[b, :, :] if isinstance(b, int) else ctx_in[bass.ds(b, 1), :, :].rearrange("o j d -> (o j) d")
                        sp.dma_start(ctx_sb[:, 0:KFULL, :],
                                     src[0:KFULL * P, :].rearrange("(p k) d -> p k d", k=KFULL)
                                     ).then_inc(ctx_loaded, 16)
                        sp.dma_start(ctx_sb[0:KLAST, KFULL, :], src[KFULL * P:J, :]).then_inc(ctx_loaded, 16)

                    def dup_queries(i, r):
                        c = slice(r % G * GC, (r % G + 1) * GC)
                        sp.wait_ge(q_hi, i * (4 * G) + (2 * r + 2))
                        sp.dma_start(QH[DH:P, c].bitcast(F32), QH[0:DH, c].bitcast(F32)).then_inc(q_dup[r % 2], 16)

                    def shift_rows(i, r):
                        sp.wait_ge(shift_ready, i * (2 * G) + (r + 1))
                        for q in range(4):
                            dst = QL[DH:DH + 1, r % G * GC:(r % G + 1) * GC].bitcast(F32).rearrange(
                                "o (j r i) -> o j r i", r=4, i=32)[:, :, q, :]
                            sp.dma_start(dst, mxT[32 * q:32 * q + GT, :]).then_inc(shift_in, 16)

                    def pair(i, last):
                        for r in range(2 * G):
                            if r % G == 0 and not (last and r >= G):
                                sp.wait_ge(ctx_used, i * 2 + (r // G + 2))
                                if not (last and r == 0):
                                    load_ctx(i * 2 + (r // G + 2))
                            events = []
                            for kt in range(KT + (r == 2 * G - 1)):
                                for job, n in numbered(last)[r * KT + kt]:
                                    if job[0] == "q":
                                        events.append((dup_queries, job[1]))
                                    if job[0] == "max" and job[2] == GMAX - 1:
                                        events.append((shift_rows, job[1]))
                            for act_on, group in events:
                                act_on(i, group)

                    sp.wait_ge(init_done, 1)
                    load_ctx(0)
                    sp.wait_ge(ctx_used, 1)
                    load_ctx(1)
                    dup_queries(0, 0)
                    dup_queries(0, 1)
                    shift_rows(0, 0)
                    with sp.Fori(0, PAIRS - 1) as i:
                        pair(i, False)
                    pair(PAIRS - 1, True)

                @block.scalar
                def _(act):
                    def evacuate(i, job, n):
                        kind, r, m = job
                        if kind in ("max",):
                            return
                        bank = MX[:, (len(PROLOGUE) + n) % 2, :]
                        free = bank_free[(len(PROLOGUE) + n) % 2]
                        act.wait_ge(job_mm, job_count(i, n))
                        if kind == "t":
                            c0, w = KCH[m]
                            nc.scalar.activation(cnT[:, c0:c0 + w], bank[:, 0:w], ACT.Identity,
                                                 scale=lnw[:, 2:3], bias=lnw[:, 3:4]).then_inc(free, 1)
                        elif kind == "kv":
                            c0, w = KCH[m]
                            nc.scalar.activation(K1[r][0:DH, c0:c0 + w], bank[0:DH, 0:w], ACT.Identity).then_inc(k_hi, 1)
                            nc.scalar.activation(VT[DH:P, c0:c0 + w], bank[DH:P, 0:w], ACT.Identity).then_inc(v_hi, 1)
                            nc.scalar.activation(K2[r][0:DH, c0:c0 + w], bank[0:DH, 0:w], ACT.Identity).then_inc(k_hi, 1)
                        elif kind == "vt":
                            a, z = VSPLIT[m]
                            turned = bank.bitcast(F16)[:, 0:(z - a) * P].rearrange("p (k d) -> p k d", d=P)
                            nc.scalar.activation(VH[:, r, a:z, 0:DH], turned[:, :, DH:P], ACT.Identity).then_inc(v_ready, 1)
                            nc.scalar.activation(VL[:, r, a:z, :], turned[:, :, 0:DH], ACT.Identity).then_inc(free, 1)
                        elif kind == "q":
                            for odd in range(2):
                                dst = QH[0:DH, r % G * GC:(r % G + 1) * GC].rearrange(
                                    "p (a o n) -> p a o n", o=2, n=N)[:, :, odd, :]
                                src = bank[DH * odd:DH * odd + DH, :].rearrange("p (a n) -> p a n", n=N)
                                nc.scalar.activation(dst, src, ACT.Identity).then_inc(q_hi, 1)
                        elif kind == "otr":
                            j0 = r % G * 2
                            nc.scalar.activation(OT[:, j0:j0 + 2, :].rearrange("p a c -> p (a c)"), bank,
                                                 ACT.Identity).then_inc(free, 1)
                        elif kind == "wo":
                            nc.scalar.activation(attnT[:, bass.ds((i * 2 + r) * N, N)], bank[:, 0:N],
                                                 ACT.Identity).then_inc(free, 1)

                    def step(i, s):
                        kp = keys_of(s % KT)
                        done = i * (2 * STEPS)
                        two = 2 * (s % 2)
                        act.wait_ge(scores_done, done + (s + 1))
                        nc.scalar.activation(S[0:kp, two, :], S[0:kp, two, :], ACT.Exp, scale=SCALE).then_inc(exp_done, 1)
                        act.wait_ge(lo_pool, FREE + done + s)
                        nc.scalar.activation(P32[0:kp, s % 2, :], S[0:kp, two + 1, :], ACT.Exp,
                                             scale=SCALE).then_inc(exp_done, 1)
                        act.wait_ge(exp_done, i * (4 * STEPS) + (2 * s + 1))
                        act.wait_ge(pv_done, PRING + done + (s - PRING + 1))
                        nc.scalar.activation(PH[0:kp, s % PRING, 0:CH], S[0:kp, two, :], ACT.Identity).then_inc(hi_done, 1)
                        act.wait_ge(exp_done, i * (4 * STEPS) + (2 * s + 2))
                        nc.scalar.activation(PH[0:kp, s % PRING, CH:GC], P32[0:kp, s % 2, :],
                                             ACT.Identity).then_inc(hi_done, 1)

                    def pair(i, last):
                        for s, jobs in enumerate(numbered(last)):
                            if s < 2 * STEPS:
                                step(i, s)
                            for job, n in jobs:
                                evacuate(i, job, n)

                    act.sem_inc(pv_done, PRING)
                    for n, job in enumerate(PROLOGUE):
                        evacuate(0, job, n - len(PROLOGUE))
                    with act.Fori(0, PAIRS - 1) as i:
                        pair(i, False)
                    pair(PAIRS - 1, True)

                @block.gpsimd
                def _(pool):
                    pool.sem_inc(lo_pool, FREE + 1)

                    def pair(i):
                        for s in range(2 * STEPS):
                            kp = keys_of(s % KT)
                            pool.wait_ge(hi_done, i * (4 * STEPS) + (2 * s + 2))
                            nc.gpsimd.tensor_tensor(PL[0:kp, s % PRING, CH:GC], P32[0:kp, s % 2, :],
                                                    PH[0:kp, s % PRING, CH:GC], ALU.subtract).then_inc(lo_pool, 1)

                    with pool.Fori(0, PAIRS) as i:
                        pair(i)

                @block.vector
                def _(dve):
                    dve.wait_ge(evac, CHUNKS)
                    dve.memset(ctx_sb[:, KFULL, :], 0.0)
                    dve.memset(QL[DH:P, :].bitcast(F32), 0.0)
                    for k in range(2):
                        dve.memset(K2[k][DH:P, :].bitcast(F32), 0.0)
                    dve.memset(VH[:, :, :, DH:DH + 1], 1.0)
                    dve.memset(mx[:, :], 0.0)
                    dve.drain()
                    for k in range(2):
                        dve.memset(K2[k][DH:DH + 1, :].bitcast(F32), 1.0)
                    dve.drain()
                    dve.sem_inc(init_done, 1)
                    dve.sem_inc(o_evac, FREE)
                    dve.sem_inc(lo_dve, FREE + 1)

                    def norm_context(b, part):
                        if part == 0:
                            dve.wait_ge(ctx_loaded, b * 32 + 32)
                        if part < 4:
                            for k in range(4 * part, min(4 * part + 4, KT)):
                                dve.bn_stats(kstats[:, k, :], ctx_sb[:, k, :])
                        elif part == 4:
                            stats_to_var(dve, KT, kstats)
                            dve.drain()
                            inverse_root(dve, KT)
                        else:
                            for k in range(4 * (part - 5), min(4 * (part - 5) + 4, KT)):
                                dve.tensor_scalar(cn[:, k, :], ctx_sb[:, k, :], mean[:, k:k + 1], rstd[:, k:k + 1],
                                                  ALU.subtract, ALU.mult).then_inc(cnormed, 1)
                            if part == 8:
                                dve.drain()
                                dve.sem_inc(ctx_used, 1)

                    def evacuate(i, job, n):
                        kind, r, m = job
                        bank = MX[:, (len(PROLOGUE) + n) % 2, :]
                        free = bank_free[(len(PROLOGUE) + n) % 2]
                        if kind == "max":
                            dve.wait_ge(job_mm, job_count(i, n))
                            dve.tensor_reduce(cm[:, m // MC, m % MC:m % MC + 1], bank[:, 0:MCHUNKS[m % MC][1]],
                                              AX.X, ALU.max).then_inc(free, 1)
                            if m == GMAX - 1:
                                group_shift(i, r)
                        elif kind == "kv":
                            c0, w = KCH[m]
                            done = job_count_of_kv(i, r, m)
                            dve.wait_ge(v_hi, done)
                            dve.tensor_tensor(VT[0:DH, c0:c0 + w], bank[DH:P, 0:w], VT[DH:P, c0:c0 + w],
                                              ALU.subtract).then_inc(v_lo, 1)
                            dve.wait_ge(k_hi, done * 2)
                            dve.tensor_tensor(K1[r][DH:P, c0:c0 + w], bank[0:DH, 0:w], K1[r][0:DH, c0:c0 + w],
                                              ALU.subtract).then_inc(free, 1)
                        elif kind == "q":
                            for odd in range(2):
                                dve.wait_ge(q_hi, i * (4 * G) + (2 * r + odd + 1))
                                cols = slice(r % G * GC, (r % G + 1) * GC)
                                dst = QL[0:DH, cols].rearrange("p (a o n) -> p a o n", o=2, n=N)[:, :, odd, :]
                                high = QH[0:DH, cols].rearrange("p (a o n) -> p a o n", o=2, n=N)[:, :, odd, :]
                                src = bank[DH * odd:DH * odd + DH, :].rearrange("p (a n) -> p a n", n=N)
                                ins = dve.tensor_tensor(dst, src, high, ALU.subtract)
                            ins.then_inc(free, 1)

                    def job_count_of_kv(i, parity, m):
                        batch = i * 2 + (1 if parity == 1 else 2)
                        return batch * NK + (m + 1)

                    def group_shift(i, r):
                        dve.drain()
                        dve.tensor_reduce(mx[:, 0:GT], cm[:, :, :], AX.X, ALU.max)
                        dve.drain()
                        dve.tensor_scalar(mx[:, 0:GT], mx[:, 0:GT], -1.0, LIFT, ALU.mult, ALU.add)
                        dve.drain()
                        if not (isinstance(i, int) and i * 2 * G + r == 0):
                            dve.wait_ge(shift_in, (i * (2 * G) + r) * 64)
                        dve.transpose(mxT[:, :], mx[:, :]).then_inc(shift_ready, 1)

                    def low_part(i, s):
                        kp = keys_of(s % KT)
                        dve.wait_ge(hi_done, i * (4 * STEPS) + (2 * s + 1))
                        dve.tensor_tensor(PL[0:kp, s % PRING, 0:CH], S[0:kp, 2 * (s % 2), :],
                                          PH[0:kp, s % PRING, 0:CH], ALU.subtract).then_inc(lo_dve, 1)

                    def divide(i, r):
                        dve.wait_ge(pv_done, PRING + i * (2 * STEPS) + (r + 1) * KT)
                        heads = O[:, :, 0:4 * (DH + 1)].rearrange("p u (i c) -> p u i c", c=DH + 1)
                        dve.reciprocal(rden[:, :, :], heads[:, :, :, DH])
                        dve.drain()
                        for u in range(2):
                            dve.tensor_tensor(
                                O_sb[:, r % 2, :, 2 * u * DH:(2 * u + 2) * DH].rearrange("p t (h d) -> p h t d", h=2),
                                heads[:, u, :, 0:DH].rearrange("p (h t) d -> p h t d", h=2),
                                rden[:, u, :].rearrange("p (h t o) -> p h t o", h=2, o=1).broadcast_to([P, 2, 2, DH]),
                                ALU.mult).then_inc(o_evac, 1)

                    def pair(i, last):
                        for s, jobs in enumerate(numbered(last)):
                            r, kt = divmod(s, KT)
                            if 1 <= s:
                                low_part(i, s - 1)
                            for k, (job, n) in enumerate(jobs):
                                if s == 2 * STEPS and job[0] == "otr":
                                    divide(i, 2 * G - 1)
                                evacuate(i, job, n)
                            if s < 2 * STEPS and kt == LAG - 1 and r >= 1:
                                divide(i, r - 1)
                            if s < 2 * STEPS and r % G == 0 and kt < 9 and not (last and r == G):
                                norm_context(i * 2 + (r // G + 1), kt)

                    for part in range(9):
                        norm_context(0, part)
                    for n, job in enumerate(PROLOGUE):
                        evacuate(0 if job[0] != "kv" else -1, job, n - len(PROLOGUE) + (JOBS if job[0] == "kv" else 0))
                    with dve.Fori(0, PAIRS - 1) as i:
                        pair(i, False)
                    pair(PAIRS - 1, True)

                @block.tensor
                def _(pe):
                    def side(i, job, n, last):
                        kind, r, m = job
                        bank = MX[:, (len(PROLOGUE) + n) % 2, :]
                        if not isinstance(i, int) or freed(i, n) > 0:
                            pe.wait_ge(bank_free[(len(PROLOGUE) + n) % 2], freed(i, n))
                        if kind == "max":
                            c0, w = MCHUNKS[m % MC]
                            col = r % G * GC + m // MC * P
                            if m == 0:
                                pe.wait_ge(q_dup[r % 2], (i * G + (r // 2 + 1)) * 16)
                            mm = pe.matmul(bank[:, 0:w], QH[:, col:col + P], K1[r // G % 2][:, c0:c0 + w],
                                           start=True, stop=True)
                        elif kind == "t":
                            c0, w = KCH[m]
                            batch = i * 2 + (1 if r == 1 else 2)
                            pe.wait_ge(cnormed, batch * KT + (c0 + w) // P)
                            for k in range(w // P):
                                mm = pe.transpose(bank[:, k * P:(k + 1) * P], cn[:, c0 // P + k, :], ident[:, :])
                        elif kind == "kv":
                            c0, w = KCH[m]
                            mm = pe.matmul(bank[:, 0:w], wkv_sb[:, :], cnT[:, c0:c0 + w], start=True, stop=True)
                        elif kind == "vt":
                            a, z = VSPLIT[m]
                            batch = i * 2 + (1 if r == 1 else 2)
                            pe.wait_ge(v_lo, batch * NK + NK)
                            for k in range(a, z):
                                mm = pe.transpose(bank.bitcast(F16)[:, (k - a) * P:(k - a + 1) * P],
                                                  VT[:, k * P:(k + 1) * P], ident16[:, :])
                        elif kind == "q":
                            batch = i * 2 + r // G
                            for a in range(2):
                                h0 = (r % G * 4 + 2 * a) * DH
                                mm = pe.matmul(bank[:, a * N:(a + 1) * N], wq_sb[:, h0:h0 + 2 * DH],
                                               xnT[:, bass.ds(batch * N, N)], start=True, stop=True)
                        elif kind == "otr":
                            pe.wait_ge(o_evac, FREE + (i * (2 * G) + (r + 1)) * 2)
                            for a in range(2):
                                for t in range(TT):
                                    mm = pe.transpose(bank[:, a * N + t * P:a * N + (t + 1) * P],
                                                      O_sb[:, r % 2, t, a * P:(a + 1) * P], ident[:, :])
                        elif kind == "wo":
                            if last is not None and m == 0:
                                pe.wait_ge(*ot_evacuated(i, last, r))
                            for j in range(H // 2):
                                mm = pe.matmul(bank[:, 0:N], wo_sb[:, j, :], OT[:, j, :],
                                               start=(j == 0), stop=(j == H // 2 - 1))
                        mm.then_inc(job_mm, 1)

                    def ot_evacuated(i, last, p):
                        n = [n for jobs in numbered(last) for job, n in jobs if job[:2] == ("otr", p * G + G - 1)][0]
                        return bank_free[(len(PROLOGUE) + n) % 2], freed(i, n) + 1

                    def scores(i, s):
                        r, kt = divmod(s, KT)
                        kp = keys_of(kt)
                        pe.wait_ge(lo_dve, FREE + i * (2 * STEPS) + s)
                        if kt == 0:
                            pe.wait_ge(shift_in, (i * (2 * G) + (r + 1)) * 64)
                        ks = slice(kt * P, kt * P + kp)
                        for u in range(2):
                            cols = slice(r % G * GC + u * CH, r % G * GC + (u + 1) * CH)
                            bank = S[0:kp, 2 * (s % 2) + u, :]
                            pe.matmul(bank, K1[r // G][:, ks], QH[:, cols], start=True, stop=False)
                            mm = pe.matmul(bank, K2[r // G][:, ks], QL[:, cols], start=False, stop=True)
                        mm.then_inc(scores_done, 1)

                    def weigh(i, s, half):
                        r, kt = divmod(s, KT)
                        p, kp = r // G, keys_of(kt)
                        if half == 0:
                            if kt == 0:
                                pe.wait_ge(o_evac, FREE + (i * (2 * G) + r) * 2)
                                if r % G == 0:
                                    pe.wait_ge(v_ready, (i * 2 + (p + 1)) * 2)
                            pe.wait_ge(lo_dve, FREE + 1 + i * (2 * STEPS) + (s + 1))
                        else:
                            pe.wait_ge(lo_pool, FREE + 1 + i * (2 * STEPS) + (s + 1))
                        for k in range(4):
                            q = slice((4 * half + k) * P, (4 * half + k + 1) * P)
                            o0 = k * (DH + 1)
                            hi, lo = PH[0:kp, s % PRING, q], PL[0:kp, s % PRING, q]
                            pe.matmul(O[:, half, o0:o0 + DH + 1], hi, VH[0:kp, p, kt, :],
                                      start=(kt == 0 and k == 0), stop=False, skip_group_check=True)
                            pe.matmul(O[:, half, o0:o0 + DH], hi, VL[0:kp, p, kt, :],
                                      start=False, stop=False, skip_group_check=True)
                            mm = pe.matmul(O[:, half, o0:o0 + DH + 1], lo, VH[0:kp, p, kt, :],
                                           start=False, stop=(kt == KT - 1), skip_group_check=True)
                        if half == 1:
                            mm.then_inc(pv_done, 1)

                    def pair(i, last):
                        for s, jobs in enumerate(numbered(last)):
                            if s < 2 * STEPS:
                                scores(i, s)
                                for half in range(2):
                                    for job, n in jobs[half:half + 1]:
                                        side(i, job, n, last)
                                    if s >= LAG:
                                        weigh(i, s - LAG, half)
                                for job, n in jobs[2:]:
                                    side(i, job, n, last)
                            else:
                                rest = [x for x in jobs if x[0][0] == "max"]
                                third = -(-len(rest) // 2)
                                for k in range(LAG):
                                    for job, n in rest[k * third:(k + 1) * third]:
                                        side(i, job, n, last)
                                    for half in range(2):
                                        weigh(i, s - LAG + k, half)
                                for job, n in jobs[len(rest):]:
                                    side(i, job, n, last)

                    pe.wait_ge(init_done, 1)
                    for n, job in enumerate(PROLOGUE):
                        prep = job[0] in ("t", "kv", "vt")
                        side(-1 if prep else 0, job, n - len(PROLOGUE) + (JOBS if prep else 0), None)
                    with pe.Fori(0, PAIRS - 1) as i:
                        pair(i, False)
                    pair(PAIRS - 1, True)

        with ExitStack() as cstack:
            def csb(name, shape, dt=F32):
                return cstack.enter_context(nc.sbuf_tensor(name, shape, dt))

            def csem(name):
                return cstack.enter_context(nc.semaphore(name))

            w1_sb = csb("w1_sb", [P, E, FF])
            w2_sb = csb("w2_sb", [P, E, FF // P, P])
            experts_in = csem("experts_in")
            silu = csb("silu", [P, FF // P, CH])
            hid = csb("hid", [P, 2, FF // P, CH])
            sumT = csb("sumT", [P, CH])
            logT = csb("logT", [E, CH])
            logits = csb("logits", [P, TILES, E])
            sel1 = csb("sel1", [P, TILES, E])
            sel2 = csb("sel2", [P, TILES, E])
            rt = csb("rt", [P, TILES, E])
            order = csb("order", [P, TILES, E])
            r1 = csb("r1", [P, TILES])
            r2 = csb("r2", [P, TILES])
            r3 = csb("r3", [P, TILES])
            cwc = csb("cwc", [P, 4, E])
            cwT = csb("cwT", [E, B * N])
            pick = csb("pick", [E, E, P])
            cwB = csb("cwB", [P, 2, CH])
            yw = csb("yw", [P, CH])
            acc = csb("acc", [P, CH])
            res = csb("res", [P, 2, 4, P])

            ff_mm, silu_done, hid_done, ff2_mm, sum_done, str_done, x1_done = (
                csem(n) for n in ("ff_mm", "silu_done", "hid_done", "ff2_mm", "sum_done", "str_done", "x1_done"))
            znormed, ztr, zevac, lt_mm, lt_evac, l_tr, l_evac = (
                csem(n) for n in ("znormed", "ztr", "zevac", "lt_mm", "lt_evac", "l_tr", "l_evac"))
            logits_shifted, exps_done, cw_copied, cw_tr, cw_evac, c_init = (
                csem(n) for n in ("logits_shifted", "exps_done", "cw_copied", "cw_tr", "cw_evac", "c_init"))
            h_mm, h_gelu, y_mm, y_used, b_mm, b_evac, acc_done, acc_tr, res_done, stored = (
                csem(n) for n in ("h_mm", "h_gelu", "y_mm", "y_used", "b_mm", "b_evac", "acc_done", "acc_tr",
                                  "res_done", "stored"))
            NB = FF // P

            with nc.Block() as block:
                @block.gpsimd
                def _(pool):
                    nc.gpsimd.memset(pick[:, :, :], 1.0)
                    for e in range(E):
                        nc.gpsimd.memset(order[:, :, e:e + 1], float(E - e))
                    pool.drain()
                    nc.gpsimd.affine_select(out=pick[:, :, :], in_=pick[:, :, :], compare_op=ALU.is_equal, fill=0.0,
                                            base=0, pattern=[[-1, E], [0, P]], channel_multiplier=1).then_inc(c_init, 1)

                @block.tensor
                def _(pe):
                    pe.sem_inc(y_mm, FREE)
                    pe.sem_inc(cw_tr, FREE)
                    pe.sem_inc(acc_tr, FREE)
                    with pe.Fori(0, CHUNKS) as c:
                        cols = xnT[:, bass.ds(c * CH, CH)]
                        pe.wait_ge(x1_done, FREE + c)
                        for j in [j for k in range(NB) for j in (NB + k, k)]:
                            pe.matmul(PS[:, j, :], ff1_sb[:, j * P:(j + 1) * P], cols,
                                      start=True, stop=True).then_inc(ff_mm, 1)
                        for k in range(NB):
                            pe.wait_ge(hid_done, FREE + c * NB + (k + 1))
                            mm = pe.matmul(PS[:, NB, :], ff2_sb[:, k, :], hid[:, 0, k, :],
                                           start=(k == 0), stop=(k == NB - 1))
                        mm.then_inc(ff2_mm, 1)
                        pe.wait_ge(sum_done, c + 1)
                        for i in range(4):
                            mm = pe.transpose(PS[:, NB + 1, i * P:(i + 1) * P], sumT[:, i * P:(i + 1) * P], ident[:, :])
                        mm.then_inc(str_done, 1)
                    for c in range(CHUNKS):
                        pe.wait_ge(znormed, c + 1)
                        if c >= 2:
                            pe.wait_ge(zevac, c - 1)
                        for i in range(4):
                            mm = pe.transpose(PS[:, c % 2, i * P:(i + 1) * P], nat[:, 4 * c + i, :], ident[:, :])
                        mm.then_inc(ztr, 1)
                        pe.wait_ge(zevac, c + 1)
                        if c >= 1:
                            pe.wait_ge(lt_evac, c)
                        pe.matmul(PS[0:E, 2, :], rwT[:, :], xnT[:, c * CH:(c + 1) * CH],
                                  start=True, stop=True).then_inc(lt_mm, 1)
                        pe.wait_ge(lt_evac, c + 1)
                        if c >= 1:
                            pe.wait_ge(l_evac, c)
                        for i in range(4):
                            mm = pe.transpose(PS[:, 3, i * E:(i + 1) * E], logT[:, i * P:(i + 1) * P], ident[0:E, 0:E])
                        mm.then_inc(l_tr, 1)
                    with pe.Fori(0, CHUNKS) as c:
                        pe.wait_ge(cw_copied, c + 1)
                        pe.wait_ge(cw_evac, FREE + c)
                        for i in range(4):
                            mm = pe.transpose(PS[0:E, 4, i * P:(i + 1) * P], cwc[:, i, :], ident[:, :])
                        mm.then_inc(cw_tr, 1)
                    pe.wait_ge(c_init, 1)
                    pe.wait_ge(experts_in, 32)
                    pe.wait_ge(cw_evac, FREE + CHUNKS)
                    with pe.Fori(0, CHUNKS) as c:
                        def expert_in(e):
                            for k in range(NB):
                                pe.wait_ge(h_gelu, FREE + c * (E * NB) + (max(e - 1, 0) * NB + k + 1 if e else 0))
                                pe.matmul(PS[:, k, :], w1_sb[:, e, k * P:(k + 1) * P], xnT[:, bass.ds(c * CH, CH)],
                                          start=True, stop=True).then_inc(h_mm, 1)

                        def expert_out(e):
                            if e >= 2:
                                pe.wait_ge(y_used, FREE + c * E + (e - 1))
                            for k in range(NB):
                                if k == NB - 1:
                                    pe.wait_ge(b_evac, FREE + c * E + e)
                                pe.wait_ge(h_gelu, FREE + c * (E * NB) + (e * NB + k + 1))
                                mm = pe.matmul(PS[:, 4 + e % 2, :], w2_sb[:, e, k, :], hid[:, e % 2, k, :],
                                               start=(k == 0), stop=(k == NB - 1))
                            mm.then_inc(y_mm, 1)
                            pe.matmul(PS[:, 6, :], pick[:, e, :], cwT[:, bass.ds(c * CH, CH)],
                                      start=True, stop=True).then_inc(b_mm, 1)

                        pe.wait_ge(y_used, FREE + c * E)
                        for e in range(E):
                            expert_in(e)
                            if e >= 1:
                                expert_out(e - 1)
                        expert_out(E - 1)
                        pe.wait_ge(acc_done, c + 1)
                        pe.wait_ge(res_done, FREE + c)
                        for i in range(4):
                            mm = pe.transpose(PS[:, 7, i * P:(i + 1) * P], acc[:, i * P:(i + 1) * P], ident[:, :])
                        mm.then_inc(acc_tr, 1)

                @block.scalar
                def _(act):
                    act.sem_inc(h_gelu, FREE)
                    act.sem_inc(b_evac, FREE)
                    act.sem_inc(cw_evac, FREE)
                    with act.Fori(0, CHUNKS) as c:
                        for k in range(NB):
                            act.wait_ge(ff_mm, c * (2 * NB) + (2 * k + 1))
                            if k == 0:
                                act.wait_ge(hid_done, FREE + c * NB)
                            nc.scalar.activation(silu[:, k, :], PS[:, NB + k, :], ACT.Silu).then_inc(silu_done, 1)
                    for c in range(CHUNKS):
                        act.wait_ge(ztr, c + 1)
                        nc.scalar.activation(xnT[:, c * CH:(c + 1) * CH], PS[:, c % 2, :],
                                             ACT.Identity).then_inc(zevac, 1)
                        act.wait_ge(lt_mm, c + 1)
                        if c >= 1:
                            act.wait_ge(l_tr, c)
                        nc.scalar.activation(logT[:, :], PS[0:E, 2, :], ACT.Identity).then_inc(lt_evac, 1)
                    act.wait_ge(logits_shifted, 1)
                    nc.scalar.activation(logits[:, :, :], logits[:, :, :], ACT.Exp).then_inc(exps_done, 1)
                    with act.Fori(0, CHUNKS) as c:
                        act.wait_ge(cw_tr, FREE + c + 1)
                        nc.scalar.activation(cwT[:, bass.ds(c * CH, CH)], PS[0:E, 4, :], ACT.Identity).then_inc(cw_evac, 1)
                    with act.Fori(0, CHUNKS) as c:
                        for e in range(E):
                            for k in range(NB):
                                act.wait_ge(h_mm, c * (E * NB) + (e * NB + k + 1))
                                if k == 0:
                                    act.wait_ge(y_mm, FREE + c * E + (e - 1 if e >= 2 else 0))
                                nc.scalar.activation(hid[:, e % 2, k, :], PS[:, k, :], ACT.Gelu).then_inc(h_gelu, 1)
                            if e >= 1:
                                act.wait_ge(b_mm, c * E + e)
                                if e >= 3:
                                    act.wait_ge(y_used, FREE + c * E + (e - 2))
                                else:
                                    act.wait_ge(y_used, FREE + c * E)
                                nc.scalar.activation(cwB[:, (e - 1) % 2, :], PS[:, 6, :], ACT.Identity).then_inc(b_evac, 1)
                        act.wait_ge(b_mm, c * E + E)
                        act.wait_ge(y_used, FREE + c * E + (E - 2))
                        nc.scalar.activation(cwB[:, (E - 1) % 2, :], PS[:, 6, :], ACT.Identity).then_inc(b_evac, 1)

                @block.vector
                def _(dve):
                    dve.wait_ge(gates_ready, 1)
                    dve.sem_inc(y_used, FREE)
                    dve.sem_inc(res_done, FREE)
                    dve.sem_inc(x1_done, FREE)
                    dve.sem_inc(hid_done, FREE)
                    with dve.Fori(0, CHUNKS) as c:
                        for k in range(NB):
                            dve.wait_ge(silu_done, c * NB + (k + 1))
                            dve.wait_ge(ff_mm, c * (2 * NB) + (2 * k + 2))
                            dve.tensor_tensor(hid[:, 0, k, :], silu[:, k, :], PS[:, k, :],
                                              ALU.mult).then_inc(hid_done, 1)
                        dve.wait_ge(ff2_mm, c + 1)
                        dve.tensor_tensor(sumT[:, :], PS[:, NB, :], attnT[:, bass.ds(c * CH, CH)],
                                          ALU.add).then_inc(sum_done, 1)
                        dve.wait_ge(str_done, c + 1)
                        rows = x_sb[:, bass.ds(c * 4, 4), :]
                        dve.scalar_tensor_tensor(out=rows, in0=PS[:, NB + 1, :].rearrange("p (t d) -> p t d", d=P),
                                                 scalar=gates[:, 0:1], in1=rows,
                                                 op0=ALU.mult, op1=ALU.add).then_inc(x1_done, 1)
                        dve.drain()
                        for i in range(4):
                            dve.bn_stats(stats[:, bass.ds(c * 4 + i, 1), :].rearrange("p o k -> p (o k)"),
                                         x_sb[:, bass.ds(c * 4 + i, 1), :].rearrange("p o k -> p (o k)"))
                    stats_to_var(dve, TILES)
                    dve.drain()
                    inverse_root(dve, TILES)
                    with dve.Fori(0, TILES // 4) as c:
                        for k in range(4):
                            ins = dve.tensor_scalar(nat[:, c * 4 + k, :], x_sb[:, c * 4 + k, :], mean[:, bass.ds(c * 4 + k, 1)],
                                                    rstd[:, bass.ds(c * 4 + k, 1)], ALU.subtract, ALU.mult)
                        ins.then_inc(znormed, 1)
                    with dve.Fori(0, CHUNKS) as c:
                        dve.wait_ge(l_tr, c + 1)
                        dve.tensor_copy(logits[:, bass.ds(c * 4, 4), :],
                                        PS[:, 3, 0:4 * E].rearrange("p (t e) -> p t e", e=E)).then_inc(l_evac, 1)
                    dve.drain()

                    def spread(v):
                        return v[:, :].rearrange("p (t o) -> p t o", o=1).broadcast_to([P, TILES, E])

                    dve.tensor_reduce(r1[:, :], logits[:, :, :], AX.X, ALU.max)
                    dve.drain()
                    dve.tensor_tensor(logits[:, :, :], logits[:, :, :], spread(r1), ALU.subtract).then_inc(logits_shifted, 1)
                    dve.wait_ge(exps_done, 1)
                    dve.wait_ge(c_init, 1)
                    dve.tensor_reduce(r1[:, :], logits[:, :, :], AX.X, ALU.add)
                    dve.drain()
                    dve.reciprocal(r2[:, :], r1[:, :])
                    dve.drain()
                    dve.tensor_tensor(rt[:, :, :], logits[:, :, :], spread(r2), ALU.mult)
                    dve.drain()

                    def top(best, sel):
                        dve.tensor_reduce(best[:, :], rt[:, :, :], AX.X, ALU.max)
                        dve.drain()
                        dve.tensor_tensor(sel[:, :, :], rt[:, :, :], spread(best), ALU.is_equal)
                        dve.drain()
                        dve.tensor_tensor(sel[:, :, :], sel[:, :, :], order[:, :, :], ALU.mult)
                        dve.drain()
                        dve.tensor_reduce(r3[:, :], sel[:, :, :], AX.X, ALU.max)
                        dve.drain()
                        dve.tensor_tensor(sel[:, :, :], sel[:, :, :], spread(r3), ALU.is_equal)
                        dve.drain()

                    top(r1, sel1)
                    dve.scalar_tensor_tensor(out=rt[:, :, :], in0=sel1[:, :, :], scalar=-4.0, in1=rt[:, :, :],
                                             op0=ALU.mult, op1=ALU.add)
                    dve.drain()
                    top(r2, sel2)
                    dve.tensor_tensor(r3[:, :], r1[:, :], r2[:, :], ALU.add)
                    dve.tensor_tensor(sel1[:, :, :], sel1[:, :, :], spread(r1), ALU.mult)
                    dve.tensor_tensor(sel2[:, :, :], sel2[:, :, :], spread(r2), ALU.mult)
                    dve.drain()
                    dve.tensor_scalar(r3[:, :], r3[:, :], 1e-9, None, ALU.add)
                    dve.tensor_tensor(sel1[:, :, :], sel1[:, :, :], sel2[:, :, :], ALU.add)
                    dve.drain()
                    dve.reciprocal(r3[:, :], r3[:, :])
                    dve.drain()
                    dve.tensor_tensor(sel1[:, :, :], sel1[:, :, :], spread(r3), ALU.mult)
                    dve.drain()
                    with dve.Fori(0, CHUNKS) as c:
                        dve.wait_ge(cw_tr, FREE + c)
                        dve.tensor_copy(cwc[:, :, :], sel1[:, bass.ds(c * 4, 4), :]).then_inc(cw_copied, 1)
                    with dve.Fori(0, CHUNKS) as c:
                        dve.wait_ge(acc_tr, FREE + c)
                        for e in range(E):
                            dve.wait_ge(y_mm, FREE + c * E + (e + 1))
                            dve.wait_ge(b_evac, FREE + c * E + (e + 1))
                            dst = acc if e == 0 else yw
                            ins = dve.tensor_tensor(dst[:, :], PS[:, 4 + e % 2, :], cwB[:, e % 2, :],
                                                    ALU.mult)
                            ins.then_inc(y_used, 1)
                            dve.drain()
                            if e:
                                ins = dve.tensor_tensor(acc[:, :], acc[:, :], yw[:, :], ALU.add)
                                if e == E - 1:
                                    ins.then_inc(acc_done, 1)
                                dve.drain()
                        dve.wait_ge(acc_tr, FREE + c + 1)
                        dve.wait_ge(stored, FREE + c * 16)
                        dve.scalar_tensor_tensor(out=res[:, 0, :, :], in0=PS[:, 7, :].rearrange("p (t d) -> p t d", d=P),
                                                 scalar=gates[:, 1:2], in1=x_sb[:, bass.ds(c * 4, 4), :],
                                                 op0=ALU.mult, op1=ALU.add).then_inc(res_done, 1)

                @block.sync
                def _(sp):
                    sp.dma_start(w1_sb[:, :, :], w1.rearrange("e d h -> d e h")).then_inc(experts_in, 16)
                    sp.dma_start(w2_sb[:, :, :, :], w2.rearrange("e (j p) d -> p e j d", p=P)).then_inc(experts_in, 16)
                    rows = out.rearrange("b n d -> (b n) d").rearrange("(t p) d -> p t d", p=P)
                    sp.sem_inc(stored, FREE)
                    with sp.Fori(0, CHUNKS) as c:
                        sp.wait_ge(res_done, FREE + c + 1)
                        sp.dma_start(rows[:, bass.ds(c * 4, 4), :], res[:, 0, :, :]).then_inc(stored, 16)
                    sp.wait_ge(stored, FREE + 16 * CHUNKS)


_INS = ['x', 'ctx_1024', 'g_xattn', 'g_ffn', 'L0_xattn_ln_g', 'L0_xattn_ln_b', 'L0_xattn_cln_g', 'L0_xattn_cln_b',
        'L0_xattn_Wq', 'L0_xattn_Wkv', 'L0_xattn_Wo', 'L0_xattn_Wff1', 'L0_xattn_Wff2', 'L0_ffn_router_w',
        'L0_ffn_w1', 'L0_ffn_w2']


def kernel(**inputs):
    import numpy as _np
    import concourse.bacc as _bacc
    from concourse import mybir as _mybir
    from concourse.bass_utils import run_bass_kernel_spmd as _run

    nc = _bacc.Bacc("TRN2", target_bir_lowering=False, num_devices=1)
    arrays, args = {}, []
    for name in _INS:
        a = _np.ascontiguousarray(inputs[name].T if name == 'L0_ffn_router_w' else inputs[name])
        arrays[f"in_{name}_dram"] = a
        args.append(nc.dram_tensor(f"in_{name}_dram", a.shape, _mybir.dt.from_np(a.dtype), kind="ExternalInput").ap())
    args.append(nc.dram_tensor("out_0_dram", (16, 256, 128), _mybir.dt.float32, kind="ExternalOutput").ap())
    build(nc, *args)
    r = _run(nc, [arrays], core_ids=[0])
    return r.results[0]["out_0_dram"]
```

```python
from contextlib import ExitStack

import concourse.bass as bass
from concourse import mybir

ALU = mybir.AluOpType
ACT = mybir.ActivationFunctionType
AX = mybir.AxisListType
F32 = mybir.dt.float32
F32R = mybir.dt.float32r
F16 = mybir.dt.float16
I32 = mybir.dt.int32

P = 128
B = 16
N = 256
J = 1601
H = 16
DH = 64
FF = 512
E = 8
EPS = 1e-5
SCALE = DH ** -0.5

TILES = B * N // P
TT = N // P
KT = -(-J // P)
KFULL = KT - 1
KLAST = J - KFULL * P
KPAD = KT * P
CH = 512
CHUNKS = B * N // CH
QCOLS = H * N
GC = 1024
G = QCOLS // GC
GT = GC // P
STEPS = G * KT
MC = 4
MCHUNKS = [(0, 400), (400, 400), (800, 400), (J - 402, 402)]
GMAX = GT * MC
PRING = 4
EXPS = 4
LAG = 2
FREE = 1
LIFT = 22.0


def keys_of(kt):
    return P if kt < KFULL else KLAST


def build(nc, x, ctx_in, g_xattn, g_ffn, ln_g, ln_b, cln_g, cln_b, Wq, Wkv, Wo, Wff1, Wff2,
          router_w, w1, w2, out):
    stack = ExitStack()
    with stack:
        def sb(name, shape, dt=F32):
            return stack.enter_context(nc.sbuf_tensor(name, shape, dt))

        def sem(name):
            return stack.enter_context(nc.semaphore(name))

        x_sb = sb("x_sb", [P, TILES, P])
        ident = sb("ident", [P, P])
        stats = sb("stats", [P, TILES, 6])
        small = sb("small", [P, 6, TILES])
        mean, var, rstd, tmp, first_var, first_rstd = (small[:, i, :] for i in range(6))
        gates = sb("gates", [P, 2])
        lnw = sb("lnw", [P, 4])
        ident16 = sb("ident16", [P, P], F16)
        bound = sb("bound", [P, 2])
        vscale = sb("vscale", [P, 2])
        rwT = sb("rwT", [P, E])

        tokens = stack.enter_context(ExitStack())
        xnT = tokens.enter_context(nc.sbuf_tensor("xnT", [P, B * N], F32))
        attnT_wide = tokens.enter_context(nc.sbuf_tensor("attnT", [P, (B + 1) * N], F32))
        attnT = attnT_wide[:, N:(B + 1) * N]
        nat = attnT.rearrange("p (t d) -> p t d", d=P)

        wq_sb, wkv_sb, wo_sb, ff1_sb, ff2_sb = (
            tokens.enter_context(nc.sbuf_tensor(n, shape, F32))
            for n, shape in (("wq_sb", [P, H * DH]), ("wkv_sb", [P, 2 * DH]), ("wo_sb", [P, H // 2, P]),
                             ("ff1_sb", [P, 2 * FF]), ("ff2_sb", [P, FF // P, P])))

        PS = stack.enter_context(nc.psum_tensor("PS", [P, 8, CH], F32))

        attention = stack.enter_context(ExitStack())
        def bsb(name, shape, dt=F32):
            return attention.enter_context(nc.sbuf_tensor(name, shape, dt))

        def bsem(name):
            return attention.enter_context(nc.semaphore(name))

        ctx_sb = bsb("ctx_sb", [P, KT, P])
        cn = bsb("cn", [P, KT, P])
        cnT = bsb("cnT", [P, KPAD])
        K1 = [bsb(f"K1_{i}", [P, KPAD], F32R) for i in range(2)]
        K2 = [bsb(f"K2_{i}", [P, KPAD], F32R) for i in range(2)]
        VT = bsb("VT", [P, KPAD], F16)
        VH = bsb("VH", [P, 2, KT, DH + 1], F16)
        VL = bsb("VL", [P, 2, KT, DH], F16)
        QH = bsb("QH", [P, QCOLS], F32R)
        QL = bsb("QL", [P, QCOLS], F32R)
        P32 = bsb("P32", [P, 2, CH])
        PH = bsb("PH", [P, PRING, GC], F16)
        PL = bsb("PL", [P, PRING, GC], F16)
        cm = bsb("cm", [P, GT, MC])
        mx = bsb("mx", [P, 32])
        mxT = bsb("mxT", [P, 32])
        rden = bsb("rden", [P, 2, 4])
        O_sb = bsb("O_sb", [P, 2, TT, G * DH])
        OT = bsb("OT", [P, H // 2, N])
        kstats = bsb("kstats", [P, KT, 6])
        kmr = bsb("kmr", [P, 2, KT])

        S = PS[:, 0:4, :]
        MX = PS[:, 4:6, :]
        O = PS[:, 6:8, :]

        ctx_loaded, kstats_ready, pad_done, cnormed = (
            bsem(n) for n in ("ctx_loaded", "kstats_ready", "pad_done", "cnormed"))
        job_mm = bsem("job_mm")
        bank_free = [bsem(f"bank_free_{i}") for i in range(2)]
        k_hi, k_dup, v_hi, v_lo, v_ready = (
            bsem(n) for n in ("k_hi", "k_dup", "v_hi", "v_lo", "v_ready"))
        q_hi, shift_ready, shift_in = (
            bsem(n) for n in ("q_hi", "shift_ready", "shift_in"))
        q_dup = [bsem(f"q_dup_{i}") for i in range(2)]
        scores_done, exp_done, lo_dve, lo_pool, pv_done, o_evac = (
            bsem(n) for n in ("scores_done", "exp_done", "lo_dve", "lo_pool", "pv_done",
                              "o_evac"))

        KCH = [(j, min(CH, KPAD - j)) for j in range(0, KPAD, CH)]
        NK = len(KCH)
        NORM_PARTS = 7

        XPARTS = 4
        XT = TILES // XPARTS
        weights_in, x_in = sem("weights_in"), [sem(f"x_in_{c}") for c in range(XPARTS)]
        consts_ready = sem("consts_ready")
        normed, tr_done, evac = sem("normed"), sem("tr_done"), sem("evac")
        gates_ready, bounds_ready = sem("gates_ready"), sem("bounds_ready")

        def stats_to_var(dve, n, st=None, eps=EPS):
            st = stats if st is None else st
            dve.drain()
            dve.tensor_tensor(mean[:, 0:n], st[:, 0:n, 1], st[:, 0:n, 4], ALU.add)
            dve.tensor_tensor(tmp[:, 0:n], st[:, 0:n, 1], st[:, 0:n, 4], ALU.subtract)
            dve.tensor_tensor(var[:, 0:n], st[:, 0:n, 2], st[:, 0:n, 5], ALU.add)
            dve.drain()
            dve.scalar_tensor_tensor(out=tmp[:, 0:n], in0=tmp[:, 0:n], scalar=0.25, in1=tmp[:, 0:n],
                                     op0=ALU.mult, op1=ALU.mult)
            dve.tensor_scalar(mean[:, 0:n], mean[:, 0:n], 0.5, None, ALU.mult)
            dve.tensor_scalar(var[:, 0:n], var[:, 0:n], 1.0 / P, eps, ALU.mult, ALU.add)
            dve.drain()
            return dve.tensor_tensor(var[:, 0:n], var[:, 0:n], tmp[:, 0:n], ALU.add)

        def root_guess(dve, n):
            dve.tensor_scalar(tmp[:, 0:n].bitcast(I32), var[:, 0:n].bitcast(I32), 1, None, ALU.logical_shift_right)
            dve.drain()
            dve.tensor_scalar(rstd[:, 0:n].bitcast(I32), tmp[:, 0:n].bitcast(I32), -1.0, float(0x5F3759DF),
                              ALU.mult, ALU.add)
            dve.drain()

        def root_step(dve, n):
            y = rstd[:, 0:n]
            dve.tensor_tensor(tmp[:, 0:n], y, y, ALU.mult)
            dve.drain()
            dve.scalar_tensor_tensor(out=tmp[:, 0:n], in0=tmp[:, 0:n], scalar=-0.5, in1=var[:, 0:n],
                                     op0=ALU.mult, op1=ALU.mult)
            dve.drain()
            dve.scalar_tensor_tensor(out=y, in0=tmp[:, 0:n], scalar=1.5, in1=y, op0=ALU.add, op1=ALU.mult)
            dve.drain()

        def inverse_root(dve, n):
            root_guess(dve, n)
            for _ in range(3):
                root_step(dve, n)

        def load_ctx(sp, b):
            src = ctx_in[b, :, :] if isinstance(b, int) else ctx_in[bass.ds(b, 1), :, :].rearrange("o j d -> (o j) d")
            sp.dma_start(ctx_sb[:, 0:KFULL, :],
                         src[0:KFULL * P, :].rearrange("(p k) d -> p k d", k=KFULL)
                         ).then_inc(ctx_loaded, 16)
            sp.dma_start(ctx_sb[0:KLAST, KFULL, :], src[KFULL * P:J, :]).then_inc(ctx_loaded, 16)

        def norm_context(dve, b, part):
            if part == 0:
                dve.wait_ge(ctx_loaded, b * 32 + 32)
            if part < 4:
                for k in range(4 * part, min(4 * part + 4, KT)):
                    dve.bn_stats(kstats[:, k, :], ctx_sb[:, k, :])
            elif part == 4:
                stats_to_var(dve, KT, kstats)
                dve.drain()
                root_guess(dve, KT)
            elif part == 5:
                root_step(dve, KT)
                root_step(dve, KT)
            else:
                root_step(dve, KT)
                dve.tensor_copy(kmr[:, 0, :], mean[:, 0:KT])
                dve.tensor_copy(kmr[:, 1, :], rstd[:, 0:KT]).then_inc(kstats_ready, 1)

        def apply_norm(pool, b, part):
            k0, k1 = 4 * part, min(4 * part + 4, KT)
            if part == 0:
                pool.wait_ge(kstats_ready, b + 1)
            both = [kmr[:, m, k0:k1].rearrange("p (t o) -> p t o", o=1).broadcast_to([P, k1 - k0, P])
                    for m in range(2)]
            nc.gpsimd.tensor_tensor(cn[:, k0:k1, :], ctx_sb[:, k0:k1, :], both[0], ALU.subtract)
            pool.drain()
            nc.gpsimd.tensor_tensor(cn[:, k0:k1, :], cn[:, k0:k1, :], both[1], ALU.mult).then_inc(cnormed, 1)

        with nc.Block() as block:
            @block.sync
            def _(sp):
                sp.wait_ge(pad_done, 1)
                load_ctx(sp, 0)
                for c in range(XPARTS):
                    sp.dma_start(x_sb[:, c * XT:(c + 1) * XT, :],
                                 x.rearrange("b n d -> (b n) d").rearrange("(t p) d -> p t d", p=P)
                                 [:, c * XT:(c + 1) * XT, :]).then_inc(x_in[c], 16)
                for k, v in enumerate((ln_g, ln_b, cln_g, cln_b)):
                    sp.dma_start(lnw[:, k:k + 1], v.rearrange("(d o) -> d o", o=1)).then_inc(weights_in, 16)
                for k, v in enumerate((g_xattn, g_ffn)):
                    sp.dma_start(gates[:, k:k + 1], v.rearrange("(o a) -> o a", o=1).broadcast_to([P, 1])
                                 ).then_inc(weights_in, 16)
                sp.dma_start(wkv_sb[:, :], Wkv).then_inc(weights_in, 16)
                sp.dma_start(wq_sb[:, :], Wq).then_inc(weights_in, 16)
                sp.dma_start(wo_sb[:, :, :], Wo.rearrange("(j p) d -> p j d", p=P)).then_inc(weights_in, 16)
                sp.dma_start(ff1_sb[:, :], Wff1).then_inc(weights_in, 16)
                sp.dma_start(ff2_sb[:, :, :], Wff2.rearrange("(j p) d -> p j d", p=P)).then_inc(weights_in, 16)
                sp.dma_start(rwT[:, :], router_w).then_inc(weights_in, 16)

            @block.gpsimd
            def _(pool):
                nc.gpsimd.memset(ident[:, :], 1.0)
                pool.drain()
                nc.gpsimd.affine_select(out=ident[:, :], in_=ident[:, :], compare_op=ALU.is_equal, fill=0.0,
                                        base=0, pattern=[[-1, P]], channel_multiplier=1).then_inc(consts_ready, 1)
                pool.drain()
                for k in range(2):
                    nc.gpsimd.memset(K2[k][DH:P, :].bitcast(F32), 0.0)
                pool.drain()
                for k in range(2):
                    nc.gpsimd.memset(K2[k][DH:DH + 1, :].bitcast(F32), 1.0)
                pool.drain()
                nc.gpsimd.memset(VH[:, :, :, DH:DH + 1], 1.0)
                for part in range(NK):
                    apply_norm(pool, 0, part)
                nc.gpsimd.memset(O_sb[:, :, :, :], 0.0)
                nc.gpsimd.memset(OT[:, :, :], 0.0)
                pool.drain()
                pool.wait_ge(bounds_ready, 1)
                nc.gpsimd.partition_all_reduce(vscale[:, :], bound[:, :], P, bass.bass_isa.ReduceOp.max).then_inc(bounds_ready, 1)

            @block.vector
            def _(dve):
                dve.memset(ctx_sb[:, KFULL, :], 0.0)
                dve.drain()
                dve.sem_inc(pad_done, 1)
                dve.memset(mx[:, :], 0.0)
                dve.memset(QL[DH:P, :].bitcast(F32), 0.0)
                for part in range(NORM_PARTS):
                    norm_context(dve, 0, part)
                for c in range(XPARTS):
                    dve.wait_ge(x_in[c], 16)
                    for t in range(c * XT, (c + 1) * XT):
                        dve.bn_stats(stats[:, t, :], x_sb[:, t, :])
                stats_to_var(dve, TILES, eps=0.0)
                dve.drain()
                dve.tensor_copy(first_var[:, :], var[:, :])
                dve.drain()
                dve.tensor_scalar(var[:, :], var[:, :], EPS, None, ALU.add)
                dve.drain()
                inverse_root(dve, TILES)
                dve.tensor_copy(first_rstd[:, :], rstd[:, :])
                dve.tensor_tensor(var[:, :], first_var[:, :], rstd[:, :], ALU.mult)
                dve.drain()
                dve.tensor_tensor(var[:, :], var[:, :], first_rstd[:, :], ALU.mult)
                dve.drain()
                dve.tensor_scalar(var[:, :], var[:, :], EPS, None, ALU.add)
                dve.drain()
                inverse_root(dve, TILES)
                dve.tensor_tensor(rstd[:, :], rstd[:, :], first_rstd[:, :], ALU.mult)
                dve.drain()
                for t in range(TILES):
                    ins = dve.tensor_scalar(nat[:, t, :], x_sb[:, t, :], mean[:, t:t + 1], rstd[:, t:t + 1],
                                            ALU.subtract, ALU.mult)
                    if t % 4 == 3:
                        ins.then_inc(normed, 1)
                dve.wait_ge(weights_in, 16 * 12)
                dve.wait_ge(consts_ready, 1)
                dve.tensor_copy(ident16[:, :], ident[:, :])
                dve.tensor_reduce(bound[:, 0:1], wkv_sb[:, DH:2 * DH], AX.X, ALU.max, apply_absolute_value=True)
                dve.tensor_reduce(bound[:, 1:2], lnw[:, 2:4], AX.X, ALU.max, apply_absolute_value=True)
                dve.drain()
                dve.sem_inc(bounds_ready, 1)
                dve.wait_ge(bounds_ready, 2)
                dve.tensor_scalar(vscale[:, :], vscale[:, :], 1e-15, None, ALU.max)
                dve.drain()
                dve.tensor_tensor(vscale[:, 0:1], vscale[:, 0:1], vscale[:, 1:2], ALU.mult)
                dve.drain()
                dve.reciprocal(vscale[:, 1:2], vscale[:, 0:1])
                dve.drain()
                dve.tensor_scalar(wkv_sb[:, DH:2 * DH], wkv_sb[:, DH:2 * DH], vscale[:, 1:2], None, ALU.mult)
                dve.tensor_scalar(wo_sb[:, :, :], wo_sb[:, :, :], vscale[:, 0:1], None, ALU.mult)

            @block.scalar
            def _(act):
                act.wait_ge(weights_in, 16 * 12)
                for c in range(CHUNKS):
                    act.wait_ge(tr_done, c + 1)
                    nc.scalar.activation(xnT[:, c * CH:(c + 1) * CH], PS[:, c, :], ACT.Identity,
                                         scale=lnw[:, 0:1], bias=lnw[:, 1:2]).then_inc(evac, 1)
                nc.scalar.activation(gates[:, :], gates[:, :], ACT.Tanh).then_inc(gates_ready, 1)

            @block.tensor
            def _(pe):
                pe.wait_ge(consts_ready, 1)
                for c in range(CHUNKS):
                    pe.wait_ge(normed, c + 1)
                    for i in range(4):
                        mm = pe.transpose(PS[:, c, i * P:(i + 1) * P], nat[:, 4 * c + i, :], ident[:, :])
                    mm.then_inc(tr_done, 1)

        VSPLIT = [(0, 7), (7, KT)]
        PAIRS = B // 2

        def prep_jobs(p):
            return ([("t", p, j) for j in range(NK)], [("kv", p, j) for j in range(NK)],
                    [("vt", p, u) for u in range(2)])

        MAX_END = 8
        PRE = KT - 1 - MAX_END
        LOAD = {"max": (8, 3, 0), "kv": (20, 14, 16), "q": (20, 14, 16), "t": (0, 6, 8), "vt": (0, 5, 14),
                "otr": (0, 7, 8), "wo": (0, 14, 5)}
        STEP_LOAD = (10, 25, 31)
        DIVIDE_LOAD = 16
        NORM_LOAD = [8, 8, 8, 4, 20, 20, 20]

        def plan():
            at = [[] for _ in range(2 * STEPS)]
            load = [list(STEP_LOAD) for _ in range(2 * STEPS)]
            for r in range(2 * G):
                p, g = divmod(r, G)
                t, kv, vt = prep_jobs(1 - p)
                for kt, job in {0: [(9, t[0]), (11, t[1])], 1: [(1, t[2]), (4, t[3]), (8, kv[0]), (11, kv[1])],
                                2: [(1, kv[2]), (4, kv[3])], 3: [(5, vt[0]), (8, vt[1])]}[g]:
                    at[r * KT + kt].append(job)
                at[r * KT + 2].append(("otr", r - 1, 0))
                if g == 0:
                    at[r * KT + 5].append(("wo", p - 1, 0))
                at[r * KT + 6].append(("q", r + 2, 0))
                load[r * KT + KT - 1][0] += DIVIDE_LOAD
                if g == 0:
                    for kt, more in enumerate(NORM_LOAD):
                        load[r * KT + kt][0] += more
            for s in range(2 * STEPS):
                for job in at[s]:
                    vector, tensor, scalar = LOAD[job[0]]
                    load[s + 1][0] += vector
                    load[s][1] += tensor
                    load[s + 1][2] += scalar
            fixed = [list(jobs) for jobs in at]
            for r in range(2 * G):
                window = range(r * KT - PRE, r * KT + MAX_END + 1)
                count = dict.fromkeys(window, 0)
                for _ in range(GMAX):
                    s = min((k for k in window if count[k] < (2 if fixed[k % (2 * STEPS)] else 4)),
                            key=lambda k: (max(load[k % (2 * STEPS)][0] + 8, load[k % (2 * STEPS)][1] + 3), k))
                    load[s % (2 * STEPS)][0] += LOAD["max"][0]
                    load[s % (2 * STEPS)][1] += LOAD["max"][1]
                    count[s] += 1
                m = 0
                for s in window:
                    for _ in range(count[s]):
                        at[s % (2 * STEPS)].append(("max", r + 1 + (2 * G if s < 0 else 0), m))
                        m += 1
            for s, jobs in enumerate(at):
                assert len(fixed[s]) <= 1 and (not fixed[s] or s + 1 < 2 * STEPS)
                if fixed[s]:
                    jobs.append(jobs.pop(0))
            return at

        def done_by_now(job):
            kind, r, m = job
            return kind in ("otr", "wo") or (kind in ("max", "q") and r < 2 * G)

        WHOLE = plan()
        ENDING = [[job for job in jobs if done_by_now(job) or (s < STEPS and job[0] in ("t", "kv", "vt"))]
                  for s, jobs in enumerate(WHOLE)] + [[("otr", 2 * G - 1, 0), ("wo", 1, 0)]]
        SIDE = {False: WHOLE, True: ENDING}
        JOBS = sum(map(len, WHOLE))
        assert JOBS % 2 == 0
        PROLOGUE = ([j for part in prep_jobs(0) for j in part] + [("q", 0, 0), ("q", 1, 0)]
                    + [("max", 0, m) for m in range(GMAX)]
                    + [("max", 1, job[2]) for jobs in WHOLE for job in jobs if job[:2] == ("max", 2 * G + 1)])

        def numbered(last):
            n, out_ = 0, []
            for jobs in SIDE[last]:
                out_.append([(job, n + k) for k, job in enumerate(jobs)])
                n += len(jobs)
            return out_

        def job_count(i, n):
            return i * JOBS + (len(PROLOGUE) + n + 1)

        def exps(i, s, k):
            return i * (2 * STEPS * EXPS) + ((s + 2) * EXPS + k)

        def freed(i, n):
            return i * (JOBS // 2) + (len(PROLOGUE) + n) // 2

        with nc.Block() as block:
            @block.sync
            def _(sp):
                def dup_queries(i, r):
                    c = slice(r % G * GC, (r % G + 1) * GC)
                    sp.wait_ge(q_hi, i * (4 * G) + (2 * r + 2))
                    sp.dma_start(QH[DH:P, c].bitcast(F32), QH[0:DH, c].bitcast(F32)).then_inc(q_dup[r % 2], 16)

                def dup_keys(i, parity, batch=None):
                    batch = i * 2 + (1 if parity == 1 else 2) if batch is None else 0
                    sp.wait_ge(k_hi, batch * NK + NK)
                    sp.dma_start(K2[parity][0:DH, :].bitcast(F32), K1[parity][0:DH, :].bitcast(F32)).then_inc(k_dup, 16)

                def shift_rows(i, r):
                    sp.wait_ge(shift_ready, i * (2 * G) + (r + 1))
                    for q in range(4):
                        dst = QL[DH:DH + 1, r % G * GC:(r % G + 1) * GC].bitcast(F32).rearrange(
                            "o (j r i) -> o j r i", r=4, i=32)[:, :, q, :]
                        sp.dma_start(dst, mxT[32 * q:32 * q + GT, :]).then_inc(shift_in, 16)

                def pair(i, last):
                    for r in range(2 * G):
                        events = []
                        for kt in range(KT):
                            for job, n in numbered(last)[r * KT + kt]:
                                if job[0] == "q":
                                    events.append((dup_queries, job[1]))
                                if job[0] == "max" and job[2] == GMAX - 1:
                                    events.append((shift_rows, job[1]))
                                if job[0] == "kv" and job[2] == NK - 1:
                                    events.append((dup_keys, job[1]))
                        for copy, which in events:
                            copy(i, which)
                        if r % G == 0 and not last:
                            sp.wait_ge(cnormed, (i * 2 + (r // G + 2)) * NK)
                            load_ctx(sp, i * 2 + (r // G + 2))

                load_ctx(sp, 1)
                dup_keys(0, 0, -1)
                dup_queries(0, 0)
                dup_queries(0, 1)
                shift_rows(0, 0)
                with sp.Fori(0, PAIRS - 1) as i:
                    pair(i, False)
                pair(PAIRS - 1, True)

            @block.scalar
            def _(act):
                def evacuate(i, job, n):
                    kind, r, m = job
                    if kind in ("max",):
                        return
                    bank = MX[:, (len(PROLOGUE) + n) % 2, :]
                    free = bank_free[(len(PROLOGUE) + n) % 2]
                    act.wait_ge(job_mm, job_count(i, n))
                    if kind == "t":
                        c0, w = KCH[m]
                        nc.scalar.activation(cnT[:, c0:c0 + w], bank[:, 0:w], ACT.Identity,
                                             scale=lnw[:, 2:3], bias=lnw[:, 3:4]).then_inc(free, 1)
                    elif kind == "kv":
                        c0, w = KCH[m]
                        nc.scalar.activation(K1[r][0:DH, c0:c0 + w], bank[0:DH, 0:w], ACT.Identity).then_inc(k_hi, 1)
                        nc.scalar.activation(VT[DH:P, c0:c0 + w], bank[DH:P, 0:w], ACT.Identity).then_inc(v_hi, 1)
                    elif kind == "vt":
                        a, z = VSPLIT[m]
                        turned = bank.bitcast(F16)[:, 0:(z - a) * P].rearrange("p (k d) -> p k d", d=P)
                        nc.scalar.activation(VH[:, r, a:z, 0:DH], turned[:, :, DH:P], ACT.Identity).then_inc(v_ready, 1)
                        nc.scalar.activation(VL[:, r, a:z, :], turned[:, :, 0:DH], ACT.Identity).then_inc(free, 1)
                    elif kind == "q":
                        for odd in range(2):
                            dst = QH[0:DH, r % G * GC:(r % G + 1) * GC].rearrange(
                                "p (a o n) -> p a o n", o=2, n=N)[:, :, odd, :]
                            src = bank[DH * odd:DH * odd + DH, :].rearrange("p (a n) -> p a n", n=N)
                            nc.scalar.activation(dst, src, ACT.Identity).then_inc(q_hi, 1)
                    elif kind == "otr":
                        j0 = r % G * 2
                        nc.scalar.activation(OT[:, j0:j0 + 2, :].rearrange("p a c -> p (a c)"), bank,
                                             ACT.Identity).then_inc(free, 1)
                    elif kind == "wo":
                        nc.scalar.activation(attnT_wide[:, bass.ds((i * 2 + r + 1) * N, N)], bank[:, 0:N],
                                             ACT.Identity).then_inc(free, 1)

                def step(i, s, jobs):
                    kp = keys_of(s % KT)
                    done = i * (2 * STEPS)
                    two = 2 * (s % 2)
                    act.wait_ge(scores_done, i * (4 * STEPS) + (2 * s + 1))
                    act.wait_ge(pv_done, PRING + done + (s - PRING + 1))
                    nc.scalar.activation(PH[0:kp, s % PRING, 0:CH], S[0:kp, two, :], ACT.Exp,
                                         scale=SCALE).then_inc(exp_done, 1)
                    nc.scalar.activation(S[0:kp, two, :], S[0:kp, two, :], ACT.Exp, scale=SCALE).then_inc(exp_done, 1)
                    act.wait_ge(scores_done, i * (4 * STEPS) + (2 * s + 2))
                    nc.scalar.activation(PH[0:kp, s % PRING, CH:GC], S[0:kp, two + 1, :], ACT.Exp,
                                         scale=SCALE).then_inc(exp_done, 1)
                    act.wait_ge(lo_pool, FREE + done + s)
                    nc.scalar.activation(P32[0:kp, s % 2, :], S[0:kp, two + 1, :], ACT.Exp,
                                         scale=SCALE).then_inc(exp_done, 1)
                    for job, n in jobs:
                        evacuate(i, job, n)

                def pair(i, last):
                    for s, jobs in enumerate(numbered(last)):
                        if not (last and s + 1 >= 2 * STEPS):
                            step(i, s + 1, numbered(last)[s - 1] if s else [])
                        elif s == 2 * STEPS:
                            for job, n in jobs:
                                evacuate(i, job, n)

                act.sem_inc(pv_done, PRING)
                act.sem_inc(exp_done, 2 * EXPS)
                for n, job in enumerate(PROLOGUE):
                    evacuate(0, job, n - len(PROLOGUE))
                step(0, 0, [])
                with act.Fori(0, PAIRS - 1) as i:
                    pair(i, False)
                pair(PAIRS - 1, True)

            @block.gpsimd
            def _(pool):
                pool.sem_inc(lo_pool, FREE + 1)
                APPLY = {8: 0, 9: 1, 10: 2, 11: 3}

                def pair(i, last):
                    for s in range(2 * STEPS):
                        r, kt = divmod(s, KT)
                        kp = keys_of(kt)
                        if r % G == 0 and kt in APPLY and not (last and r == G):
                            apply_norm(pool, i * 2 + (r // G + 1), APPLY[kt])
                        pool.wait_ge(exp_done, exps(i, s, EXPS))
                        nc.gpsimd.tensor_tensor(PL[0:kp, s % PRING, CH:GC], P32[0:kp, s % 2, :],
                                                PH[0:kp, s % PRING, CH:GC], ALU.subtract).then_inc(lo_pool, 1)

                with pool.Fori(0, PAIRS - 1) as i:
                    pair(i, False)
                pair(PAIRS - 1, True)

            @block.vector
            def _(dve):
                dve.sem_inc(o_evac, FREE)
                dve.sem_inc(lo_dve, FREE + 1)

                def evacuate(i, job, n):
                    kind, r, m = job
                    bank = MX[:, (len(PROLOGUE) + n) % 2, :]
                    free = bank_free[(len(PROLOGUE) + n) % 2]
                    if kind == "max":
                        dve.wait_ge(job_mm, job_count(i, n))
                        dve.tensor_reduce(cm[:, m // MC, m % MC:m % MC + 1], bank[:, 0:MCHUNKS[m % MC][1]],
                                          AX.X, ALU.max).then_inc(free, 1)
                        if m == GMAX - 1:
                            group_shift(i, r)
                    elif kind == "kv":
                        c0, w = KCH[m]
                        done = job_count_of_kv(i, r, m)
                        dve.wait_ge(v_hi, done)
                        dve.tensor_tensor(VT[0:DH, c0:c0 + w], bank[DH:P, 0:w], VT[DH:P, c0:c0 + w],
                                          ALU.subtract).then_inc(v_lo, 1)
                        dve.wait_ge(k_hi, done)
                        dve.tensor_tensor(K1[r][DH:P, c0:c0 + w], bank[0:DH, 0:w], K1[r][0:DH, c0:c0 + w],
                                          ALU.subtract).then_inc(free, 1)
                    elif kind == "q":
                        for odd in range(2):
                            dve.wait_ge(q_hi, i * (4 * G) + (2 * r + odd + 1))
                            cols = slice(r % G * GC, (r % G + 1) * GC)
                            dst = QL[0:DH, cols].rearrange("p (a o n) -> p a o n", o=2, n=N)[:, :, odd, :]
                            high = QH[0:DH, cols].rearrange("p (a o n) -> p a o n", o=2, n=N)[:, :, odd, :]
                            src = bank[DH * odd:DH * odd + DH, :].rearrange("p (a n) -> p a n", n=N)
                            ins = dve.tensor_tensor(dst, src, high, ALU.subtract)
                        ins.then_inc(free, 1)

                def job_count_of_kv(i, parity, m):
                    batch = i * 2 + (1 if parity == 1 else 2)
                    return batch * NK + (m + 1)

                def group_shift(i, r):
                    dve.drain()
                    dve.tensor_reduce(mx[:, 0:GT], cm[:, :, :], AX.X, ALU.max)
                    dve.drain()
                    dve.tensor_scalar(mx[:, 0:GT], mx[:, 0:GT], -1.0, LIFT, ALU.mult, ALU.add)
                    dve.drain()
                    if not (isinstance(i, int) and i * 2 * G + r == 0):
                        dve.wait_ge(shift_in, (i * (2 * G) + r) * 64)
                    dve.transpose(mxT[:, :], mx[:, :]).then_inc(shift_ready, 1)

                def low_part(i, s):
                    kp = keys_of(s % KT)
                    dve.wait_ge(exp_done, exps(i, s, 2))
                    dve.tensor_tensor(PL[0:kp, s % PRING, 0:CH], S[0:kp, 2 * (s % 2), :],
                                      PH[0:kp, s % PRING, 0:CH], ALU.subtract).then_inc(lo_dve, 1)

                def divide(i, r):
                    dve.wait_ge(pv_done, PRING + i * (2 * STEPS) + (r + 1) * KT)
                    heads = O[:, :, 0:4 * (DH + 1)].rearrange("p u (i c) -> p u i c", c=DH + 1)
                    dve.reciprocal(rden[:, :, :], heads[:, :, :, DH])
                    dve.drain()
                    for u in range(2):
                        dve.tensor_tensor(
                            O_sb[:, r % 2, :, 2 * u * DH:(2 * u + 2) * DH].rearrange("p t (h d) -> p h t d", h=2),
                            heads[:, u, :, 0:DH].rearrange("p (h t) d -> p h t d", h=2),
                            rden[:, u, :].rearrange("p (h t o) -> p h t o", h=2, o=1).broadcast_to([P, 2, 2, DH]),
                            ALU.mult).then_inc(o_evac, 1)

                def pair(i, last):
                    for s, jobs in enumerate(numbered(last)):
                        r, kt = divmod(s, KT)
                        if not (last and s + 1 >= 2 * STEPS):
                            low_part(i, s + 1)
                        jobs = [x for x in jobs if x[0][0] == "max"]
                        before = [x for x in (numbered(last)[s - 1] if s else []) if x[0][0] != "max"]
                        for job, n in jobs[:1] + before + jobs[1:]:
                            evacuate(i, job, n)
                        if s < 2 * STEPS and kt == KT - 1:
                            divide(i, r)
                        if s < 2 * STEPS and r % G == 0 and kt < 7 and not (last and r == G):
                            norm_context(dve, i * 2 + (r // G + 1), kt)

                for n, job in enumerate(PROLOGUE):
                    evacuate(0 if job[0] != "kv" else -1, job, n - len(PROLOGUE) + (JOBS if job[0] == "kv" else 0))
                low_part(0, 0)
                with dve.Fori(0, PAIRS - 1) as i:
                    pair(i, False)
                pair(PAIRS - 1, True)

            @block.tensor
            def _(pe):
                def side(i, job, n, last):
                    kind, r, m = job
                    bank = MX[:, (len(PROLOGUE) + n) % 2, :]
                    if not isinstance(i, int) or freed(i, n) > 0:
                        pe.wait_ge(bank_free[(len(PROLOGUE) + n) % 2], freed(i, n))
                    if kind == "max":
                        c0, w = MCHUNKS[m % MC]
                        col = r % G * GC + m // MC * P
                        if m == 0:
                            pe.wait_ge(q_dup[r % 2], (i * G + (r // 2 + 1)) * 16)
                        mm = pe.matmul(bank[:, 0:w], QH[:, col:col + P], K1[r // G % 2][:, c0:c0 + w],
                                       start=True, stop=True)
                    elif kind == "t":
                        c0, w = KCH[m]
                        batch = i * 2 + (1 if r == 1 else 2)
                        pe.wait_ge(cnormed, batch * NK + (m + 1))
                        for k in range(w // P):
                            mm = pe.transpose(bank[:, k * P:(k + 1) * P], cn[:, c0 // P + k, :], ident[:, :])
                    elif kind == "kv":
                        c0, w = KCH[m]
                        mm = pe.matmul(bank[:, 0:w], wkv_sb[:, :], cnT[:, c0:c0 + w], start=True, stop=True)
                    elif kind == "vt":
                        a, z = VSPLIT[m]
                        batch = i * 2 + (1 if r == 1 else 2)
                        pe.wait_ge(v_lo, batch * NK + NK)
                        for k in range(a, z):
                            mm = pe.transpose(bank.bitcast(F16)[:, (k - a) * P:(k - a + 1) * P],
                                              VT[:, k * P:(k + 1) * P], ident16[:, :])
                    elif kind == "q":
                        batch = i * 2 + r // G
                        for a in range(2):
                            h0 = (r % G * 4 + 2 * a) * DH
                            mm = pe.matmul(bank[:, a * N:(a + 1) * N], wq_sb[:, h0:h0 + 2 * DH],
                                           xnT[:, bass.ds(batch * N, N)], start=True, stop=True)
                    elif kind == "otr":
                        pe.wait_ge(o_evac, FREE + (i * (2 * G) + (r + 1)) * 2)
                        for a in range(2):
                            for t in range(TT):
                                mm = pe.transpose(bank[:, a * N + t * P:a * N + (t + 1) * P],
                                                  O_sb[:, r % 2, t, a * P:(a + 1) * P], ident[:, :])
                    elif kind == "wo":
                        if last is not None and m == 0:
                            pe.wait_ge(*ot_evacuated(i, last, r))
                        for j in range(H // 2):
                            mm = pe.matmul(bank[:, 0:N], wo_sb[:, j, :], OT[:, j, :],
                                           start=(j == 0), stop=(j == H // 2 - 1))
                    mm.then_inc(job_mm, 1)

                def ot_evacuated(i, last, p):
                    n = [n for jobs in numbered(last) for job, n in jobs if job[:2] == ("otr", p * G + G - 1)][0]
                    return bank_free[(len(PROLOGUE) + n) % 2], freed(i, n) + 1

                def scores(i, s):
                    r, kt = divmod(s, KT)
                    kp = keys_of(kt)
                    if kt == 0 and r % G == 0:
                        pe.wait_ge(k_dup, (i * 2 + (r // G + 1)) * 16)
                    if kt == 0:
                        pe.wait_ge(shift_in, (i * (2 * G) + (r + 1)) * 64)
                    ks, p = slice(kt * P, kt * P + kp), r // G % 2
                    for u in range(2):
                        cols = slice(r % G * GC + u * CH, r % G * GC + (u + 1) * CH)
                        bank = S[0:kp, 2 * (s % 2) + u, :]
                        if u == 0:
                            pe.wait_ge(lo_dve, FREE + i * (2 * STEPS) + s)
                        else:
                            pe.wait_ge(exp_done, exps(i, s - 2, EXPS))
                        pe.matmul(bank, K1[p][:, ks], QH[:, cols], start=True, stop=False)
                        mm = pe.matmul(bank, K2[p][:, ks], QL[:, cols], start=False, stop=True)
                        mm.then_inc(scores_done, 1)

                def weigh(i, s, half):
                    r, kt = divmod(s, KT)
                    p, kp = r // G, keys_of(kt)
                    if kt == 0:
                        pe.wait_ge(o_evac, (i * (2 * G) + r) * 2 + (FREE + half - 1))
                    if half == 0:
                        if kt == 0 and r % G == 0:
                            pe.wait_ge(v_ready, (i * 2 + (p + 1)) * 2)
                        pe.wait_ge(lo_dve, FREE + 1 + i * (2 * STEPS) + (s + 1))
                    else:
                        pe.wait_ge(lo_pool, FREE + 1 + i * (2 * STEPS) + (s + 1))
                    for k in range(4):
                        q = slice((4 * half + k) * P, (4 * half + k + 1) * P)
                        o0 = k * (DH + 1)
                        hi, lo = PH[0:kp, s % PRING, q], PL[0:kp, s % PRING, q]
                        pe.matmul(O[:, half, o0:o0 + DH + 1], hi, VH[0:kp, p, kt, :],
                                  start=(kt == 0 and k == 0), stop=False, skip_group_check=True)
                        pe.matmul(O[:, half, o0:o0 + DH], hi, VL[0:kp, p, kt, :],
                                  start=False, stop=False, skip_group_check=True)
                        mm = pe.matmul(O[:, half, o0:o0 + DH + 1], lo, VH[0:kp, p, kt, :],
                                       start=False, stop=(kt == KT - 1), skip_group_check=True)
                    if half == 1:
                        mm.then_inc(pv_done, 1)

                def pair(i, last):
                    for s, jobs in enumerate(numbered(last)):
                        if not (last and s + LAG >= 2 * STEPS):
                            scores(i, s + LAG)
                        maxes = sum(job[0] == "max" for job, n in jobs)
                        projected = s and any(job[0] in ("kv", "q") for job, n in numbered(last)[s - 1])
                        first = min(1 if projected else 2, maxes)
                        for job, n in jobs[:first]:
                            side(i, job, n, last)
                        if s < 2 * STEPS:
                            weigh(i, s, 0)
                            weigh(i, s, 1)
                        for job, n in jobs[first:]:
                            side(i, job, n, last)

                for n, job in enumerate(PROLOGUE):
                    prep = job[0] in ("t", "kv", "vt")
                    side(-1 if prep else 0, job, n - len(PROLOGUE) + (JOBS if prep else 0), None)
                for s in range(LAG):
                    scores(0, s)
                with pe.Fori(0, PAIRS - 1) as i:
                    pair(i, False)
                pair(PAIRS - 1, True)

        attention.close()

        NB = FF // P
        with ExitStack() as cstack:
            silu = cstack.enter_context(nc.sbuf_tensor("silu", [P, NB, CH], F32))
            hid = cstack.enter_context(nc.sbuf_tensor("hid", [P, NB, CH], F32))
            sumT = cstack.enter_context(nc.sbuf_tensor("sumT", [P, CH], F32))
            ff_mm, silu_done, hid_done, ff2_mm, sum_done, str_done, x1_done = (
                cstack.enter_context(nc.semaphore(n))
                for n in ("ff_mm", "silu_done", "hid_done", "ff2_mm", "sum_done", "str_done", "x1_done"))
            SUM, STR = 4, 5

            with nc.Block() as block:
                @block.tensor
                def _(pe):
                    pe.sem_inc(ff2_mm, NB)

                    def first(c, k):
                        pe.wait_ge(hid_done, 2 + c * NB + (k - 1))
                        cols = xnT[:, bass.ds(c * CH, CH)]
                        for j, bank in ((NB + k, 2 * (k % 2)), (k, 2 * (k % 2) + 1)):
                            pe.matmul(PS[:, bank, :], ff1_sb[:, j * P:(j + 1) * P], cols,
                                      start=True, stop=True).then_inc(ff_mm, 1)

                    def second(c, k):
                        if k == 0:
                            pe.wait_ge(sum_done, FREE + c)
                        pe.wait_ge(hid_done, 2 + c * NB + (k + 1))
                        pe.matmul(PS[:, SUM, :], ff2_sb[:, k, :], hid[:, k, :],
                                  start=(k == 0), stop=(k == NB - 1)).then_inc(ff2_mm, 1)

                    def turn_sum(c):
                        pe.wait_ge(sum_done, FREE + c + 1)
                        pe.wait_ge(x1_done, FREE + c)
                        for i in range(4):
                            mm = pe.transpose(PS[:, STR, i * P:(i + 1) * P], sumT[:, i * P:(i + 1) * P], ident[:, :])
                        mm.then_inc(str_done, 1)

                    for k in range(NB):
                        first(0, k)
                    for k in range(NB):
                        first(1, k)
                        second(0, k)
                    with pe.Fori(0, CHUNKS - 2) as i:
                        for k in range(NB):
                            first(i + 2, k)
                            if k == 0:
                                turn_sum(i)
                            second(i + 1, k)
                    turn_sum(CHUNKS - 2)
                    for k in range(NB):
                        second(CHUNKS - 1, k)
                    turn_sum(CHUNKS - 1)

                @block.scalar
                def _(act):
                    with act.Fori(0, CHUNKS) as c:
                        for k in range(NB):
                            act.wait_ge(ff_mm, c * (2 * NB) + (2 * k + 1))
                            act.wait_ge(hid_done, 1 + c * NB + k)
                            nc.scalar.activation(silu[:, k, :], PS[:, 2 * (k % 2), :], ACT.Silu).then_inc(silu_done, 1)

                @block.vector
                def _(dve):
                    dve.wait_ge(gates_ready, 1)
                    dve.sem_inc(x1_done, FREE)
                    dve.sem_inc(sum_done, FREE)
                    dve.sem_inc(hid_done, 2)

                    def gate(c, k):
                        dve.wait_ge(silu_done, c * NB + (k + 1))
                        dve.wait_ge(ff_mm, c * (2 * NB) + (2 * k + 2))
                        dve.wait_ge(ff2_mm, c * NB + (k + 1))
                        dve.tensor_tensor(hid[:, k, :], silu[:, k, :], PS[:, 2 * (k % 2) + 1, :],
                                          ALU.mult).then_inc(hid_done, 1)

                    def add_up(c):
                        dve.wait_ge(ff2_mm, NB + c * NB + NB)
                        dve.tensor_tensor(sumT[:, :], PS[:, SUM, :], attnT[:, bass.ds(c * CH, CH)],
                                          ALU.add).then_inc(sum_done, 1)

                    def residual(c):
                        dve.wait_ge(str_done, c + 1)
                        rows = x_sb[:, bass.ds(c * 4, 4), :]
                        dve.scalar_tensor_tensor(out=rows, in0=PS[:, STR, :].rearrange("p (t d) -> p t d", d=P),
                                                 scalar=gates[:, 0:1], in1=rows,
                                                 op0=ALU.mult, op1=ALU.add).then_inc(x1_done, 1)
                        dve.drain()
                        for i in range(4):
                            dve.bn_stats(stats[:, bass.ds(c * 4 + i, 1), :].rearrange("p o k -> p (o k)"),
                                         x_sb[:, bass.ds(c * 4 + i, 1), :].rearrange("p o k -> p (o k)"))

                    for k in range(NB):
                        gate(0, k)
                    for k in range(NB):
                        gate(1, k)
                    add_up(0)
                    with dve.Fori(0, CHUNKS - 2) as i:
                        gate(i + 2, 0)
                        gate(i + 2, 1)
                        residual(i)
                        gate(i + 2, 2)
                        gate(i + 2, 3)
                        add_up(i + 1)
                    residual(CHUNKS - 2)
                    add_up(CHUNKS - 1)
                    residual(CHUNKS - 1)

        tokens.close()

        with ExitStack() as dstack:
            def dsb(name, shape, dt=F32):
                return dstack.enter_context(nc.sbuf_tensor(name, shape, dt))

            def dsem(name):
                return dstack.enter_context(nc.semaphore(name))

            w1_raw = dsb("w1_raw", [P, 2, FF])
            w2_raw = dsb("w2_raw", [P, 2, NB, P])
            w1_lo = dsb("w1_lo", [P, E, FF], F32R)
            w2_lo = dsb("w2_lo", [P, E, NB, P], F32R)
            w1_hi = dsb("w1_hi", [P, E, FF], F32R)
            w2_hi = dsb("w2_hi", [P, E, NB, P], F32R)
            z_hi = dsb("z_hi", [P, B * N], F32R)
            z_lo = dsb("z_lo", [P, B * N], F32R)
            zn = dsb("zn", [P, 8, P])
            rw_hi = dsb("rw_hi", [P, E], F32R)
            rw_lo = dsb("rw_lo", [P, E], F32R)
            hid_hi = dsb("hid_hi", [P, 2, NB, CH], F32R)
            hid_lo = dsb("hid_lo", [P, 2, NB, CH], F32R)
            logits = dsb("logits", [P, TILES, E])
            sel1 = dsb("sel1", [P, TILES, E])
            sel2 = dsb("sel2", [P, TILES, E])
            rt = dsb("rt", [P, TILES, E])
            order = dsb("order", [P, TILES, E])
            r1 = dsb("r1", [P, TILES])
            r2 = dsb("r2", [P, TILES])
            r3 = dsb("r3", [P, TILES])
            cwc = dsb("cwc", [P, TILES, 2 * E])
            cwT = dsb("cwT", [2 * E, B * N], F32R)
            pick = dsb("pick", [2 * E, E, P], F32R)
            cwB = dsb("cwB", [P, 2, CH])
            logT = cwB[0:E, :, :]
            sums = dsb("sums", [P, 2, CH])
            acc, yw = sums[:, 0, :], sums[:, 1, :]
            pick32 = sums[0:2 * E, :, :].rearrange("p a (b c) -> p (a b) c", c=P)
            res = dsb("res", [P, 4, P])

            w1_in, w2_in = ([dsem(f"{n}_{i}") for i in range(2)] for n in ("w1_in", "w2_in"))
            w_hi, w_lo, rw_split = (dsem(n) for n in ("w_hi", "w_lo", "rw_split"))
            znormed, ztr, zh_done, zl_done, lt_mm, lt_evac, l_tr = (
                dsem(n) for n in ("znormed", "ztr", "zh_done", "zl_done", "lt_mm", "lt_evac", "l_tr"))
            logits_shifted, exps_done, cw_ready, cw_tr, cw_evac, c_init = (
                dsem(n) for n in ("logits_shifted", "exps_done", "cw_ready", "cw_tr", "cw_evac", "c_init"))
            h_mm, h_gelu, h_lo, y_mm, y_used, b_mm, b_evac, acc_done, acc_tr, res_done, stored = (
                dsem(n) for n in ("h_mm", "h_gelu", "h_lo", "y_mm", "y_used", "b_mm", "b_evac", "acc_done",
                                  "acc_tr", "res_done", "stored"))
            LOGITS = 6
            Y, PICK, OUTT = 4, 6, 7

            with nc.Block() as block:
                @block.sync
                def _(sp):
                    for e in range(E):
                        if e >= 2:
                            sp.wait_ge(w_lo, 2 * e - 2)
                        sp.dma_start(w1_raw[:, e % 2, :], w1[e, :, :]).then_inc(w1_in[e % 2], 16)
                        sp.dma_start(w2_raw[:, e % 2, :, :],
                                     w2[e, :, :].rearrange("(j p) d -> p j d", p=P)).then_inc(w2_in[e % 2], 16)
                    rows = out.rearrange("b n d -> (b n) d").rearrange("(t p) d -> p t d", p=P)
                    sp.sem_inc(stored, FREE)
                    with sp.Fori(0, CHUNKS) as c:
                        sp.wait_ge(res_done, FREE + c + 1)
                        sp.dma_start(rows[:, bass.ds(c * 4, 4), :], res[:, :, :]).then_inc(stored, 16)
                    sp.wait_ge(stored, FREE + 16 * CHUNKS)

                @block.gpsimd
                def _(pool):
                    nc.gpsimd.tensor_copy(rw_hi[:, :], rwT[:, :])
                    pool.drain()
                    nc.gpsimd.tensor_tensor(rw_lo[:, :], rwT[:, :], rw_hi[:, :], ALU.subtract).then_inc(rw_split, 1)
                    pool.drain()
                    nc.gpsimd.memset(pick32[:, :, :], 0.0)
                    for e in range(E):
                        nc.gpsimd.memset(order[:, :, e:e + 1], float(E - e))
                    for k in range(2):
                        pool.drain()
                        nc.gpsimd.affine_select(out=pick32[:, :, :], in_=pick32[:, :, :], compare_op=ALU.not_equal,
                                                fill=1.0, base=-k * E, pattern=[[-1, E], [0, P]],
                                                channel_multiplier=1)
                    pool.drain()
                    nc.gpsimd.tensor_copy(pick[:, :, :], pick32[:, :, :]).then_inc(c_init, 1)
                    pool.drain()
                    for e in range(E):
                        pool.wait_ge(w_hi, 2 * e + 1)
                        nc.gpsimd.tensor_tensor(w1_lo[:, e, :], w1_raw[:, e % 2, :], w1_hi[:, e, :],
                                                ALU.subtract).then_inc(w_lo, 1)
                        pool.wait_ge(w_hi, 2 * e + 2)
                        nc.gpsimd.tensor_tensor(w2_lo[:, e, :, :], w2_raw[:, e % 2, :, :], w2_hi[:, e, :, :],
                                                ALU.subtract).then_inc(w_lo, 1)

                @block.tensor
                def _(pe):
                    pe.sem_inc(y_mm, 2)
                    pe.sem_inc(acc_tr, FREE)

                    for t in range(CHUNKS + 2):
                        if t < CHUNKS:
                            pe.wait_ge(znormed, t + 1)
                            if t >= 4:
                                pe.wait_ge(zl_done, t - 3)
                            for i in range(4):
                                mm = pe.transpose(PS[:, t % 4, i * P:(i + 1) * P], zn[:, 4 * (t % 2) + i, :], ident[:, :])
                            mm.then_inc(ztr, 1)
                        c = t - 1
                        if 0 <= c < CHUNKS:
                            pe.wait_ge(zl_done, c + 1)
                            if c == 0:
                                pe.wait_ge(rw_split, 1)
                            if c >= 2:
                                pe.wait_ge(lt_evac, c - 1)
                            cols = slice(c * CH, (c + 1) * CH)
                            for j, (w, z) in enumerate(((rw_hi, z_hi), (rw_hi, z_lo), (rw_lo, z_hi))):
                                mm = pe.matmul(PS[0:E, 4 + c % 2, :], w[:, :], z[:, cols], start=(j == 0), stop=(j == 2))
                            mm.then_inc(lt_mm, 1)
                        c = t - 2
                        if c >= 0:
                            pe.wait_ge(lt_evac, c + 1)
                            for i in range(4):
                                mm = pe.transpose(PS[:, LOGITS, (4 * c + i) * E:(4 * c + i + 1) * E],
                                                  logT[:, c % 2, i * P:(i + 1) * P], ident[0:E, 0:E])
                            mm.then_inc(l_tr, 1)
                    pe.wait_ge(cw_ready, 1)
                    for c in range(CHUNKS):
                        for i in range(4):
                            mm = pe.transpose(PS[0:2 * E, c, i * P:(i + 1) * P], cwc[:, 4 * c + i, :],
                                              ident[:, :])
                        mm.then_inc(cw_tr, 1)

                    def expert_in(c, e):
                        for k in range(NB):
                            pe.wait_ge(h_lo, c * (E * NB) + (e * NB + k + 1))
                            for j, (w, z) in enumerate(((w1_hi[:, e, k * P:(k + 1) * P], z_hi),
                                                        (w1_hi[:, e, k * P:(k + 1) * P], z_lo),
                                                        (w1_lo[:, e, k * P:(k + 1) * P], z_hi))):
                                mm = pe.matmul(PS[:, k, :], w, z[:, bass.ds(c * CH, CH)], start=(j == 0), stop=(j == 2))
                            mm.then_inc(h_mm, 1)

                    def expert_out(c, e):
                        pe.wait_ge(y_used, c * E + (e + 1))
                        for k in range(NB):
                            pe.wait_ge(h_lo, NB + c * (E * NB) + (e * NB + k + 1))
                            for j, (w, h) in enumerate(((w2_hi[:, e, k, :], hid_hi), (w2_hi[:, e, k, :], hid_lo),
                                                        (w2_lo[:, e, k, :], hid_hi))):
                                if k == NB - 1 and j == 2:
                                    pe.wait_ge(b_evac, FREE + c * E + e)
                                mm = pe.matmul(PS[:, Y + e % 2, :], w, h[:, e % 2, k, :],
                                               start=(k == 0 and j == 0), stop=(k == NB - 1 and j == 2))
                        mm.then_inc(y_mm, 1)
                        pe.matmul(PS[:, PICK, :], pick[:, e, :], cwT[:, bass.ds(c * CH, CH)],
                                  start=True, stop=True).then_inc(b_mm, 1)

                    def chunk(c, last):
                        for e in range(E - 1):
                            expert_in(c, e + 1)
                            expert_out(c, e)
                        expert_out(c, E - 1)
                        if not last:
                            expert_in(c + 1, 0)
                        pe.wait_ge(acc_done, c + 1)
                        pe.wait_ge(res_done, FREE + c)
                        for i in range(4):
                            mm = pe.transpose(PS[:, OUTT, i * P:(i + 1) * P], acc[:, i * P:(i + 1) * P], ident[:, :])
                        mm.then_inc(acc_tr, 1)

                    pe.wait_ge(c_init, 1)
                    pe.wait_ge(w_lo, 2 * E)
                    pe.wait_ge(cw_evac, CHUNKS)
                    expert_in(0, 0)
                    with pe.Fori(0, CHUNKS - 1) as c:
                        chunk(c, False)
                    chunk(CHUNKS - 1, True)

                @block.scalar
                def _(act):
                    act.sem_inc(b_evac, FREE)
                    for t in range(CHUNKS + 1):
                        if t < CHUNKS:
                            act.wait_ge(ztr, t + 1)
                            nc.scalar.activation(z_hi[:, t * CH:(t + 1) * CH], PS[:, t % 4, :],
                                                 ACT.Identity).then_inc(zh_done, 1)
                            if t:
                                for e in range(t - 1, t + t // (CHUNKS - 1)):
                                    act.wait_ge(w1_in[e % 2], e // 2 * 16 + 16)
                                    nc.scalar.activation(w1_hi[:, e, :], w1_raw[:, e % 2, :], ACT.Identity).then_inc(w_hi, 1)
                                    act.wait_ge(w2_in[e % 2], e // 2 * 16 + 16)
                                    nc.scalar.activation(w2_hi[:, e, :, :], w2_raw[:, e % 2, :, :],
                                                         ACT.Identity).then_inc(w_hi, 1)
                        c = t - 1
                        if c >= 0:
                            act.wait_ge(lt_mm, c + 1)
                            if c >= 2:
                                act.wait_ge(l_tr, c - 1)
                            nc.scalar.activation(logT[:, c % 2, :], PS[0:E, 4 + c % 2, :],
                                                 ACT.Identity).then_inc(lt_evac, 1)
                    act.wait_ge(logits_shifted, 1)
                    nc.scalar.activation(logits[:, :, :], logits[:, :, :], ACT.Exp).then_inc(exps_done, 1)
                    for c in range(CHUNKS):
                        act.wait_ge(cw_tr, c + 1)
                        nc.scalar.activation(cwT[:, c * CH:(c + 1) * CH], PS[0:2 * E, c, :],
                                             ACT.Identity).then_inc(cw_evac, 1)

                    def gelus(c, e):
                        for k in range(NB):
                            act.wait_ge(h_mm, c * (E * NB) + (e * NB + k + 1))
                            if k == 0:
                                act.wait_ge(y_mm, c * E + (e + 1))
                            nc.scalar.activation(hid_hi[:, e % 2, k, :], PS[:, k, :], ACT.Gelu).then_inc(h_gelu, 1)
                            nc.scalar.activation(PS[:, k, :], PS[:, k, :], ACT.Gelu).then_inc(h_gelu, 1)

                    def combine_weight(c, e):
                        act.wait_ge(b_mm, c * E + (e + 1))
                        act.wait_ge(y_used, c * E + (e + 1))
                        nc.scalar.activation(cwB[:, e % 2, :], PS[:, PICK, :], ACT.Identity).then_inc(b_evac, 1)

                    def chunk(c, last):
                        for e in range(E - 1):
                            gelus(c, e + 1)
                            combine_weight(c, e)
                        combine_weight(c, E - 1)
                        if not last:
                            gelus(c + 1, 0)

                    gelus(0, 0)
                    with act.Fori(0, CHUNKS - 1) as c:
                        chunk(c, False)
                    chunk(CHUNKS - 1, True)

                @block.vector
                def _(dve):
                    dve.sem_inc(y_used, 2)
                    dve.sem_inc(res_done, FREE)
                    dve.sem_inc(h_lo, NB)
                    stats_to_var(dve, TILES)
                    dve.drain()
                    inverse_root(dve, TILES)
                    for t in range(CHUNKS + 1):
                        if t < CHUNKS:
                            if t >= 2:
                                dve.wait_ge(ztr, t - 1)
                            for i in range(4 * t, 4 * t + 4):
                                ins = dve.tensor_scalar(zn[:, i % 8, :], x_sb[:, i, :], mean[:, i:i + 1],
                                                        rstd[:, i:i + 1], ALU.subtract, ALU.mult)
                            ins.then_inc(znormed, 1)
                        c = t - 1
                        if c >= 0:
                            dve.wait_ge(zh_done, c + 1)
                            dve.tensor_tensor(z_lo[:, c * CH:(c + 1) * CH], PS[:, c % 4, :],
                                              z_hi[:, c * CH:(c + 1) * CH], ALU.subtract).then_inc(zl_done, 1)
                    dve.wait_ge(l_tr, CHUNKS)
                    first_logits = PS[:, LOGITS, 0:TILES * E].rearrange("p (t e) -> p t e", e=E)

                    def spread(v):
                        return v[:, :].rearrange("p (t o) -> p t o", o=1).broadcast_to([P, TILES, E])

                    dve.tensor_reduce(r1[:, :], first_logits, AX.X, ALU.max)
                    dve.drain()
                    dve.tensor_tensor(logits[:, :, :], first_logits, spread(r1), ALU.subtract).then_inc(logits_shifted, 1)
                    dve.wait_ge(exps_done, 1)
                    dve.wait_ge(c_init, 1)
                    dve.tensor_reduce(r1[:, :], logits[:, :, :], AX.X, ALU.add)
                    dve.drain()
                    dve.reciprocal(r2[:, :], r1[:, :])
                    dve.drain()
                    dve.tensor_tensor(rt[:, :, :], logits[:, :, :], spread(r2), ALU.mult)
                    dve.drain()

                    def top(best, sel):
                        dve.tensor_reduce(best[:, :], rt[:, :, :], AX.X, ALU.max)
                        dve.drain()
                        dve.tensor_tensor(sel[:, :, :], rt[:, :, :], spread(best), ALU.is_equal)
                        dve.drain()
                        dve.tensor_tensor(sel[:, :, :], sel[:, :, :], order[:, :, :], ALU.mult)
                        dve.drain()
                        dve.tensor_reduce(r3[:, :], sel[:, :, :], AX.X, ALU.max)
                        dve.drain()
                        dve.tensor_tensor(sel[:, :, :], sel[:, :, :], spread(r3), ALU.is_equal)
                        dve.drain()

                    top(r1, sel1)
                    dve.scalar_tensor_tensor(out=rt[:, :, :], in0=sel1[:, :, :], scalar=-4.0, in1=rt[:, :, :],
                                             op0=ALU.mult, op1=ALU.add)
                    dve.drain()
                    top(r2, sel2)
                    dve.tensor_tensor(r3[:, :], r1[:, :], r2[:, :], ALU.add)
                    dve.tensor_tensor(sel1[:, :, :], sel1[:, :, :], spread(r1), ALU.mult)
                    dve.tensor_tensor(sel2[:, :, :], sel2[:, :, :], spread(r2), ALU.mult)
                    dve.drain()
                    dve.tensor_scalar(r3[:, :], r3[:, :], 1e-9, None, ALU.add)
                    dve.tensor_tensor(sel1[:, :, :], sel1[:, :, :], sel2[:, :, :], ALU.add)
                    dve.drain()
                    dve.reciprocal(r3[:, :], r3[:, :])
                    dve.drain()
                    dve.tensor_tensor(sel1[:, :, :], sel1[:, :, :], spread(r3), ALU.mult)
                    dve.drain()
                    dve.tensor_copy(cwc[:, :, 0:E].bitcast(F32R), sel1[:, :, :])
                    dve.drain()
                    dve.tensor_tensor(cwc[:, :, E:2 * E], sel1[:, :, :], cwc[:, :, 0:E], ALU.subtract).then_inc(cw_ready, 1)

                    def low_parts(c, e):
                        for k in range(NB):
                            dve.wait_ge(h_gelu, c * (2 * E * NB) + (2 * (e * NB + k) + 2))
                            dve.tensor_tensor(hid_lo[:, e % 2, k, :], PS[:, k, :], hid_hi[:, e % 2, k, :],
                                              ALU.subtract).then_inc(h_lo, 1)

                    def weighted(c, e):
                        if e == 0:
                            dve.wait_ge(acc_tr, FREE + c)
                        dve.wait_ge(y_mm, 2 + c * E + (e + 1))
                        dve.wait_ge(b_evac, FREE + c * E + (e + 1))
                        dst = yw if e else acc
                        dve.tensor_tensor(dst[:, :], PS[:, Y + e % 2, :], cwB[:, e % 2, :], ALU.mult).then_inc(y_used, 1)
                        dve.drain()
                        if e:
                            ins = dve.tensor_tensor(acc[:, :], acc[:, :], yw[:, :], ALU.add)
                            if e == E - 1:
                                ins.then_inc(acc_done, 1)
                            dve.drain()

                    def chunk(c, last):
                        for e in range(E - 1):
                            low_parts(c, e + 1)
                            weighted(c, e)
                        weighted(c, E - 1)
                        if not last:
                            low_parts(c + 1, 0)
                        dve.wait_ge(acc_tr, FREE + c + 1)
                        dve.wait_ge(stored, FREE + c * 16)
                        dve.scalar_tensor_tensor(out=res[:, :, :], in0=PS[:, OUTT, :].rearrange("p (t d) -> p t d", d=P),
                                                 scalar=gates[:, 1:2], in1=x_sb[:, bass.ds(c * 4, 4), :],
                                                 op0=ALU.mult, op1=ALU.add).then_inc(res_done, 1)

                    low_parts(0, 0)
                    with dve.Fori(0, CHUNKS - 1) as c:
                        chunk(c, False)
                    chunk(CHUNKS - 1, True)


_INS = ['x', 'ctx_1024', 'g_xattn', 'g_ffn', 'L0_xattn_ln_g', 'L0_xattn_ln_b', 'L0_xattn_cln_g', 'L0_xattn_cln_b',
        'L0_xattn_Wq', 'L0_xattn_Wkv', 'L0_xattn_Wo', 'L0_xattn_Wff1', 'L0_xattn_Wff2', 'L0_ffn_router_w',
        'L0_ffn_w1', 'L0_ffn_w2']


def kernel(**inputs):
    import numpy as _np
    import concourse.bacc as _bacc
    from concourse import mybir as _mybir
    from concourse.bass_utils import run_bass_kernel_spmd as _run

    nc = _bacc.Bacc("TRN2", target_bir_lowering=False, num_devices=1)
    arrays, args = {}, []
    for name in _INS:
        a = _np.ascontiguousarray(inputs[name].T if name == 'L0_ffn_router_w' else inputs[name])
        arrays[f"in_{name}_dram"] = a
        args.append(nc.dram_tensor(f"in_{name}_dram", a.shape, _mybir.dt.from_np(a.dtype), kind="ExternalInput").ap())
    args.append(nc.dram_tensor("out_0_dram", (16, 256, 128), _mybir.dt.float32, kind="ExternalOutput").ap())
    build(nc, *args)
    r = _run(nc, [arrays], core_ids=[0])
    return r.results[0]["out_0_dram"]
```
